# Optimizing a Trainium2 kernel written in Bass

```python
import numpy as np
import jax
import jax.numpy as jnp

def _softmax(x, axis=-1):
    return jax.nn.softmax(x, axis=axis)

def _gelu(x):
    return jax.nn.gelu(x, approximate=True)

def _silu(x):
    return jax.nn.silu(x)

def _sigmoid(x):
    return jax.nn.sigmoid(x)

def _layernorm(x, axis=-1, eps=1e-05):
    m = jnp.mean(x, axis=axis, keepdims=True)
    v = jnp.var(x, axis=axis, keepdims=True)
    return (x - m) / jnp.sqrt(v + eps)

def _scatter_add(tgt, idx, src, axis=0):
    return tgt.at[idx].add(src)

def _segment_sum(src, seg, n):
    return jax.ops.segment_sum(src, seg, n)
kernel_name = 'mk_seq_postln_d1_jaxref_r4_3c2fb0'

def setup_inputs(seed: int=0):
    np.random.seed(seed)
    _w = jnp.asarray

    def _L0_attn_setup():
        import jax, jax.numpy as jnp
        import numpy as np
        import math
        B, T, C = (2, 512, 256)
        H = 16
        D = C // H

        def alibi_slopes(n_heads):
            start = 2.0 ** (-2.0 ** (-(math.log2(n_heads) - 3)))
            return jnp.asarray([start * start ** i for i in range(n_heads)], dtype=jnp.float32)
        key = jax.random.key(seed)
        ks = jax.random.split(key, 6)
        x = jax.random.normal(ks[0], (B, T, C), dtype=jnp.float32)
        W_attn = jax.random.normal(ks[1], (C, 3 * C), dtype=jnp.float32) * 0.02
        b_attn = jnp.zeros((3 * C,), dtype=jnp.float32)
        W_proj = jax.random.normal(ks[2], (C, C), dtype=jnp.float32) * 0.02
        b_proj = jnp.zeros((C,), dtype=jnp.float32)
        temperature = jnp.ones((1,), dtype=jnp.float32) * 2.0
        return {'x': x, 'W_attn': W_attn, 'b_attn': b_attn, 'W_proj': W_proj, 'b_proj': b_proj, 'temperature': temperature}
    _L0_attn_in = _L0_attn_setup()

    def _L0_ffn_setup():
        import jax, jax.numpy as jnp
        import numpy as np
        EPS = 1e-05

        @jax.custom_vjp
        def ste_quantize(w):
            scale = jnp.maximum(jnp.mean(jnp.abs(w)), EPS)
            return jnp.clip(jnp.round(w / scale), -1.0, 1.0)

        def _ste_fwd(w):
            return (ste_quantize(w), None)

        def _ste_bwd(_, g):
            return (g,)
        ste_quantize.defvjp(_ste_fwd, _ste_bwd)
        key = jax.random.key(seed)
        k1, k2 = jax.random.split(key)
        x = jax.random.normal(k1, (8, 2048, 256), dtype=jnp.float32)
        weight = jax.random.normal(k2, (256, 256), dtype=jnp.float32) * 0.02
        return {'x': x, 'weight': weight}
    _L0_ffn_in = _L0_ffn_setup()
    _d = {'L0_attn_x': _L0_attn_in['x'], 'L0_attn_W_attn': _L0_attn_in['W_attn'], 'L0_attn_b_attn': _L0_attn_in['b_attn'], 'L0_attn_W_proj': _L0_attn_in['W_proj'], 'L0_attn_b_proj': _L0_attn_in['b_proj'], 'L0_attn_temperature': _L0_attn_in['temperature'], 'L0_ffn_weight': _L0_ffn_in['weight']}
    _x0 = _d['L0_attn_x']
    _d['L0_attn_x'] = jax.random.normal(jax.random.fold_in(jax.random.key(seed), 1), (4, 2048, 256), dtype=_x0.dtype)
    del _x0
    return _d

def reference(L0_attn_x, L0_attn_W_attn, L0_attn_b_attn, L0_attn_W_proj, L0_attn_b_proj, L0_attn_temperature, L0_ffn_weight):

    def _L0_attn_ref(x, W_attn, b_attn, W_proj, b_proj, temperature):
        import jax, jax.numpy as jnp
        import numpy as np
        import math
        B, T, C = (2, 512, 256)
        H = 16
        D = C // H

        def alibi_slopes(n_heads):
            start = 2.0 ** (-2.0 ** (-(math.log2(n_heads) - 3)))
            return jnp.asarray([start * start ** i for i in range(n_heads)], dtype=jnp.float32)
        Bc, Tc, Cc = x.shape
        qkv = x @ W_attn + b_attn
        q, k, v = jnp.split(qkv, 3, axis=-1)
        q = q.reshape(Bc, Tc, H, D)
        k = k.reshape(Bc, Tc, H, D)
        v = v.reshape(Bc, Tc, H, D)
        scale = 1.0 / math.sqrt(D)
        att = jnp.einsum('bqhd,bkhd->bhqk', q, k) * scale
        att = att / temperature
        pos = jnp.arange(Tc, dtype=jnp.float32)
        rel = pos[None, :] - pos[:, None]
        slopes = alibi_slopes(H)
        bias = slopes[:, None, None] * rel[None, :, :]
        causal = pos[None, :] <= pos[:, None]
        bias = jnp.where(causal[None, :, :], bias, -jnp.inf)
        att = att + bias[None, :, :, :]
        w = jax.nn.softmax(att, axis=-1)
        y = jnp.einsum('bhqk,bkhd->bqhd', w, v).reshape(Bc, Tc, Cc)
        return y @ W_proj + b_proj

    def _L0_ffn_ref(x, weight):
        import jax, jax.numpy as jnp
        import numpy as np
        EPS = 1e-05

        @jax.custom_vjp
        def ste_quantize(w):
            scale = jnp.maximum(jnp.mean(jnp.abs(w)), EPS)
            return jnp.clip(jnp.round(w / scale), -1.0, 1.0)

        def _ste_fwd(w):
            return (ste_quantize(w), None)

        def _ste_bwd(_, g):
            return (g,)
        ste_quantize.defvjp(_ste_fwd, _ste_bwd)
        w_ternary = ste_quantize(weight)
        scale = jnp.maximum(jnp.mean(jnp.abs(weight)), EPS)
        return jnp.einsum('bsi,oi->bso', x, w_ternary * scale)
    x = L0_attn_x
    x = _layernorm(x + _L0_attn_ref(x, L0_attn_W_attn, L0_attn_b_attn, L0_attn_W_proj, L0_attn_b_proj, L0_attn_temperature), axis=-1)
    x = _layernorm(x + _L0_ffn_ref(x, L0_ffn_weight), axis=-1)
    return x

_drawn_inputs = setup_inputs


def setup_inputs(seed=0):
    import zlib

    import numpy as np

    out = dict(_drawn_inputs(seed))
    spreads = {'L0_attn_b_attn': (0.0, 0.1), 'L0_attn_b_proj': (0.0, 0.1)}
    factors = {}
    for name, (base, spread) in spreads.items():
        noise = np.random.default_rng([zlib.crc32(name.encode()), seed]).standard_normal(out[name].shape)
        drawn = base * np.exp(spread * noise) if base else spread * noise
        out[name] = jnp.asarray(drawn.astype(out[name].dtype))
    for name, factor in factors.items():
        out[name] = (out[name] * factor).astype(out[name].dtype)
    return out
```

```python
from contextlib import ExitStack

import numpy as np
import concourse.bass as bass
from concourse import mybir

F32 = mybir.dt.float32
BF16 = mybir.dt.bfloat16
ALU = mybir.AluOpType
ACT = mybir.ActivationFunctionType
AX = mybir.AxisListType

P = 128
B, T, C, H = 4, 2048, 256, 16
D = C // H
HG = 4
ITERS = B * H // HG
CH = 512
NG = T // CH
BLK = CH // P
NT = T // P
KC = C // P
PARTS = 3
PAIRS = [(0, 0), (1, 0), (2, 0), (0, 1), (1, 1), (0, 2)]
ALIBI_ROW = len(PAIRS) * D
ALIBI_ROWS = PARTS * NG
MAX_ROW = ALIBI_ROW + ALIBI_ROWS
ROWS = MAX_ROW + PARTS
NEG = -1.0e30
EPS = 1e-5
OUT_ROWS = 2 * D
VW = HG * OUT_ROWS


def constants(bf16):
    start = 2.0 ** (-2.0 ** (-(np.log2(H) - 3)))
    slopes = np.array([start * start ** i for i in range(H)]).astype(np.float32)
    centre = np.arange(NG, dtype=np.float32) * CH + CH // 2
    rest = (slopes[None, :, None] * (np.arange(T, dtype=np.float32)[None, None, :] - centre[:, None, None])).astype(np.float32)
    alibi = []
    for _ in range(PARTS):
        alibi.append(rest.astype(bf16))
        rest = rest - alibi[-1].astype(np.float32)
    in_chunk = np.arange(T)[None, :] // CH == np.arange(NG)[:, None]
    fixed_rows = np.concatenate([in_chunk] * PARTS + [np.ones((PARTS, T), bool)]).astype(bf16)
    mask = np.zeros((P, CH), np.float32)
    mask[:, CH - P:] = np.triu(np.full((P, P), NEG, np.float32), 1)
    alibi = np.tile(np.concatenate(alibi), (1, B, 1))
    return alibi, fixed_rows, mask[:, CH - P:].astype(bf16), mask, np.eye(P, dtype=np.float32)


def pass2_tiles(g):
    steps = []
    for i in range(BLK * g):
        steps.append([[(j, i, 0, CH, (j % 2) * CH) for j in (2 * s, 2 * s + 1)] for s in range(2)])
    d = BLK * g
    steps.append([[(j, d, 0, CH, (j % 2) * CH) for j in (2 * s, 2 * s + 1)] for s in range(2)])
    steps.append([[piece for j in (2 * s, 2 * s + 1) for piece in
                   ((j, d + 1, P, CH - P, (j % 2) * CH), (j, d + 3, 3 * P, P, (j % 2) * CH + CH - P))]
                  for s in range(2)])
    steps.append([[(j, d + 2, 2 * P, 2 * P, j * 2 * P) for j in range(HG)]])
    return steps


ORDER = list(reversed(range(NG)))
STEPS = [(g, n, step) for g in ORDER for n, step in enumerate(pass2_tiles(g))]
TILES = sum(len(step) for _, _, step in STEPS)
STRIPS = [(j, t, s) for j in range(HG) for t in range(NT) for s in range(t // BLK + 1)]
NSTRIPS = len(STRIPS)
DIAGS = HG * NT
QUIET_FIRST, QUIET_LAST = 3, 4


def strips_at(step):
    n = len(STEPS) - QUIET_FIRST - QUIET_LAST
    k = step - QUIET_FIRST
    if k < 0 or k >= n:
        return range(0)
    return range(NSTRIPS * k // n, NSTRIPS * (k + 1) // n)


STEPS_OF = {g: len(pass2_tiles(g)) for g in ORDER}
LAST_TILE = {g: sum(len(step) for gg, _, step in STEPS if ORDER.index(gg) <= ORDER.index(g)) - 1 for g in ORDER}

SCORE_SLOTS, PROB_SLOTS, STRIP_SLOTS, OUT_SLOTS = 2, 4, 2, 2
STACK_DMAS = 2 * len(PAIRS) + 1
TURN_STEP = len(STEPS) - 3


class Work:

    def __init__(self, nc, ctx):
        self.nc, self.ctx = nc, ctx

    def sb(self, name, shape, dtype=F32):
        return self.ctx.enter_context(self.nc.sbuf_tensor(name, shape, dtype))

    def psum(self, name, shape, dtype=F32):
        return self.ctx.enter_context(self.nc.psum_tensor(name, shape, dtype))

    def sem(self, name):
        return self.ctx.enter_context(self.nc.semaphore(name))

    def sems(self, name, n):
        return [self.sem(f"{name}{i}") for i in range(n)]


def row_to_all(vector, n):
    return vector.rearrange("(a n) -> a n", a=1).broadcast_to([P, n])


def build_project(nc, keep, io, scr, w_ternary):
    with ExitStack() as ctx:
        m = Work(nc, ctx)
        w = m.sb("w_attn", [P, KC, 3 * C])
        b_qk = m.sb("b_qk", [P, 2 * KC])
        b_v = m.sb("b_v", [P, C])
        temp = m.sb("temp", [P, 1])
        temp_inv = m.sb("temp_inv", [P, 1])
        scale = m.sb("scale", [P, 1])
        b_q = m.sb("b_q_scaled", [P, KC])
        w_ffn = m.sb("w_ffn", [P, KC, C])
        ones = m.sb("ones", [P, P])
        abs_sum = m.sb("abs_sum", [P, 1])
        w_scale = m.sb("w_scale", [P, 1])
        half = m.sb("half_scale", [P, 2])
        below = m.sb("below", [P, KC, C])
        above = m.sb("above", [P, KC, C])
        xt = m.sb("xt", [P, 2, KC, CH])
        full = m.sb("full", [P, 4, CH])
        rest = m.sb("rest", [P, 2, CH])
        parts = m.sb("parts", [P, 2, PARTS, 4, CH], BF16)
        vx = m.sb("vx", [P, 2, HG, BLK, VW])
        p_qk = [m.psum(f"p_qk{o}", [P, CH]) for o in range(4)]
        p_v = [m.psum(f"p_v{h}", [P, 2, C]) for h in range(2)]
        p_sum = m.psum("p_sum", [P, 1])

        w_in, ffn_in = keep.sem("w_loaded"), keep.sem("ffn_weight_loaded")
        xt_in = keep.sems("xt_loaded", 2)
        ones_ready = keep.sem("ones_ready")
        abs_ready, total_ready = keep.sem("abs_sum_ready"), keep.sem("total_ready")
        prep = keep.sem("preparation_steps")
        qk_ready, qk_free = keep.sems("qk_sums_ready", 4), keep.sems("qk_bank_free", 4)
        v_ready, v_free = keep.sems("v_sums_ready", 2), keep.sems("v_bank_free", 2)
        full_ready = keep.sem("full_ready")
        rest_ready, part2_ready = keep.sem("rest_ready"), keep.sem("part2_ready")
        parts_ready = keep.sems("parts_ready", 4)
        stored = keep.sems("scratch_stored", 2)
        STORES = 5

        block = ctx.enter_context(nc.Block())

        def load_xt(sp, n, u):
            sp.dma_start(xt[:, u], io["x_t"].rearrange("(k p) t -> p k t", p=P)[:, :, bass.ds(n * CH, CH)]).then_inc(xt_in[u], 16)

        @block.sync
        def _(sp):
            for u in range(2):
                sp.sem_inc(stored[u], 16 * STORES)
            sp.dma_start(w[:], io["w_attn"].rearrange("(k p) n -> p k n", p=P)).then_inc(w_in, 16)
            for u in range(2):
                load_xt(sp, u, u)
            sp.dma_start(b_qk[:], io["b_qk"]).then_inc(w_in, 16)
            sp.dma_start(b_v[:], row_to_all(io["b_v"], C)).then_inc(w_in, 16)
            sp.dma_start(temp[:], row_to_all(io["temperature"], 1)).then_inc(w_in, 16)
            sp.dma_start(w_ffn[:], io["w_ffn_t"].rearrange("(k p) n -> p k n", p=P)).then_inc(ffn_in, 16)

            def batch(b, last):
                for c in range(NG):
                    u = c % 2
                    for o in range(4):
                        sp.wait_ge(parts_ready[o], b * NG + c + 1 + 1)
                        dst = (scr["q"] if o < KC else scr["k"])[:, bass.ds(b * C + (o % KC) * P, P), c * CH:(c + 1) * CH]
                        sp.dma_start(dst.rearrange("s r t -> r s t"), parts[:, u, :, o, :]).then_inc(stored[u], 16)
                    for h in range(2):
                        sp.wait_ge(v_free[h], b * NG + c + 1 + 1)
                    dst = scr["v"][bass.ds(b * HG, HG), :, c * BLK:(c + 1) * BLK, :].rearrange("g p a e -> p g (a e)")
                    sp.dma_start(dst, vx[:, u].rearrange("p g a e -> p g (a e)")).then_inc(stored[u], 16)
                    if not (last and c >= NG - 2):
                        load_xt(sp, b * NG + c + 2, u)

            with sp.Fori(0, B - 1) as b:
                batch(b, False)
            batch(B - 1, True)
            for u in range(2):
                sp.wait_ge(stored[u], 16 * STORES * (B * NG // 2 + 1))

        @block.tensor
        def _(pe):
            pe.wait_ge(w_in, 64)
            pe.wait_ge(ones_ready, 1)
            pe.wait_ge(abs_ready, 1)
            pe.matmul(p_sum[:], ones[:], abs_sum[:], start=True, stop=True).then_inc(total_ready, 1)
            with pe.Fori(0, B) as b:
                for c in range(NG):
                    u = c % 2
                    pe.wait_ge(xt_in[u], b * (16 * NG // 2) + 16 * (c // 2 + 1))
                    for o in range(4):
                        pe.wait_ge(qk_free[o], b * NG + c + 1)
                        for k in range(KC):
                            mm = pe.matmul(p_qk[o][:], w[:, k, o * P:(o + 1) * P], xt[:, u, k, :], start=(k == 0), stop=(k == KC - 1))
                        mm.then_inc(qk_ready[o], 1)
                    for a in range(BLK):
                        if a % 2 == 0:
                            pe.wait_ge(v_free[a // 2], b * NG + c + 1)
                        for k in range(KC):
                            mm = pe.matmul(p_v[a // 2][:, a % 2], xt[:, u, k, a * P:(a + 1) * P], w[:, k, 2 * C:3 * C],
                                           start=(k == 0), stop=(k == KC - 1))
                        if a % 2 == 1:
                            mm.then_inc(v_ready[a // 2], 1)

        @block.scalar
        def _(act):
            for o in range(4):
                act.sem_inc(qk_free[o], 1)
            act.wait_ge(w_in, 64)
            act.wait_ge(prep, 3)
            with act.Fori(0, B) as b:
                for c in range(NG):
                    u = c % 2
                    act.wait_ge(stored[u], b * (16 * STORES * NG // 2) + 16 * STORES * (c // 2 + 1))
                    for o in range(4):
                        act.wait_ge(qk_ready[o], b * NG + c + 1)
                        act.wait_ge(parts_ready[o], b * NG + c + 1)
                        sc, bi = (scale[:, 0:1], b_q[:, o:o + 1]) if o < KC else (1.0, b_qk[:, o:o + 1])
                        act.activation(full[:, o], p_qk[o][:], ACT.Identity, bias=bi, scale=sc).then_inc(full_ready, 1)
                        act.activation(parts[:, u, 0, o], p_qk[o][:], ACT.Identity, bias=bi, scale=sc).then_inc(qk_free[o], 1)

        @block.vector
        def _(dve):
            for o in range(4):
                dve.sem_inc(parts_ready[o], 1)
            for h in range(2):
                dve.sem_inc(v_free[h], 1)
            dve.memset(ones[:], 1.0).then_inc(ones_ready, 1)
            dve.memset(vx[:], 1.0).then_inc(ones_ready, 1)
            dve.wait_ge(w_in, 64)
            dve.reciprocal(temp_inv[:], temp[:]).then_inc(prep, 1)
            dve.wait_ge(prep, 1)
            dve.tensor_scalar(scale[:], temp_inv[:], D ** -0.5, None, ALU.mult).then_inc(prep, 1)
            dve.wait_ge(prep, 2)
            dve.tensor_scalar(b_q[:], b_qk[:, 0:KC], scale[:, 0:1], None, ALU.mult).then_inc(prep, 1)
            dve.wait_ge(ffn_in, 16)
            dve.tensor_reduce(abs_sum[:], w_ffn[:], AX.XY, ALU.add, apply_absolute_value=True).then_inc(abs_ready, 1)
            dve.wait_ge(total_ready, 1)
            dve.tensor_scalar(w_scale[:], p_sum[:], 1.0 / (C * C), EPS, ALU.mult, ALU.max).then_inc(prep, 1)
            dve.wait_ge(prep, 4)
            dve.tensor_scalar(half[:, 0:1], w_scale[:], 0.5, None, ALU.mult).then_inc(prep, 1)
            dve.tensor_scalar(half[:, 1:2], w_scale[:], -0.5, None, ALU.mult).then_inc(prep, 1)
            dve.wait_ge(prep, 6)
            dve.tensor_scalar(above[:], w_ffn[:], half[:, 0:1], w_scale[:, 0:1], ALU.is_gt, ALU.mult).then_inc(prep, 1)
            dve.tensor_scalar(below[:], w_ffn[:], half[:, 1:2], w_scale[:, 0:1], ALU.is_lt, ALU.mult).then_inc(prep, 1)
            dve.wait_ge(prep, 8)
            dve.tensor_tensor(w_ternary[:], above[:], below[:], ALU.subtract).then_inc(prep, 1)
            dve.wait_ge(ones_ready, 2)
            with dve.Fori(0, B) as b:
                for c in range(NG):
                    u = c % 2
                    for o in range(4):
                        dve.wait_ge(qk_free[o], b * NG + c + 1 + 1)
                        dve.wait_ge(parts_ready[(o + 2) % 4], b * NG + c + 1 + (o >= 2))
                        dve.tensor_tensor(rest[:, o % 2], full[:, o], parts[:, u, 0, o], ALU.subtract).then_inc(rest_ready, 1)
                        dve.wait_ge(rest_ready, b * (4 * NG) + 4 * c + o + 1)
                        dve.tensor_copy(parts[:, u, 1, o], rest[:, o % 2]).then_inc(part2_ready, 1)
                        dve.wait_ge(part2_ready, b * (4 * NG) + 4 * c + o + 1)
                        dve.tensor_tensor(parts[:, u, 2, o], rest[:, o % 2], parts[:, u, 1, o], ALU.subtract).then_inc(parts_ready[o], 1)
                    dve.wait_ge(stored[u], b * (16 * STORES * NG // 2) + 16 * STORES * (c // 2 + 1))
                    for a in range(BLK):
                        dve.wait_ge(v_ready[a // 2], b * NG + c + 1)
                        dst = vx[:, u, :, a, :].rearrange("p g (j e) -> p g j e", e=OUT_ROWS)[:, :, :, 0:D]
                        add = dve.tensor_tensor(dst, p_v[a // 2][:, a % 2].rearrange("p (g j e) -> p g j e", g=HG, e=D),
                                                b_v[:].rearrange("p (g j e) -> p g j e", g=HG, e=D), ALU.add)
                        if a % 2 == 1:
                            add.then_inc(v_free[a // 2], 1)


def build_attend(nc, keep, io, scr):
    with ExitStack() as ctx:
        m = Work(nc, ctx)
        q_stack = [m.sb(f"q_stack{u}", [P, HG, T], BF16) for u in range(2)]
        k_stack = [m.sb(f"k_stack{u}", [P, HG, T], BF16) for u in range(2)]
        v_ext = [m.sb(f"v_ext{u}", [P, NT, VW]) for u in range(2)]
        probs = [m.sb(f"probs{i}", [P, 2 * CH]) for i in range(PROB_SLOTS)]
        out_sb = [m.sb(f"out_sb{i}", [P, CH]) for i in range(OUT_SLOTS)]
        mask = m.sb("mask", [P, CH])
        tri = m.sb("tri", [P, P], BF16)
        ident = m.sb("ident", [P, P], BF16)
        unused = [m.sb(f"unused{i}", [P, CH], BF16) for i in range(2)]
        strip_max = m.sb("strip_max", [P, HG * NT, NG])
        neg_max = m.sb("neg_max", [P, HG * NT])
        max_rest = m.sb("max_rest", [P, HG * NT])
        max_parts = m.sb("max_parts", [P, PARTS, HG * NT], BF16)
        max_t = m.sb("max_t", [HG * NT, PARTS, P], BF16)
        p_strip = m.psum("p_strip", [P, STRIP_SLOTS, CH])
        p_score = [m.psum(f"p_score{i}", [P, 2 * CH]) for i in range(SCORE_SLOTS)]
        p_out = [m.psum(f"p_out{i}", [P, CH]) for i in range(OUT_SLOTS)]
        p_max = p_strip[0:HG * NT, 0, 0:PARTS * P // 2].bitcast(BF16)

        const_in = keep.sem("constants_loaded")
        stack_in = [keep.sems(f"stack{u}_columns_loaded", NG) for u in range(2)]
        v_in = keep.sems("v_loaded", 2)
        max_in = keep.sem("max_rows_loaded")
        strip_ready, strip_free = keep.sems("strip_ready", STRIP_SLOTS), keep.sems("strip_bank_free", STRIP_SLOTS)
        strip_max_set = keep.sem("strip_max_set")
        max_step = keep.sem("max_steps")
        max_turned, max_copied = keep.sem("max_turned"), keep.sem("max_copied")
        score_ready = keep.sem("score_ready")
        exp_done = keep.sems("exp_done", SCORE_SLOTS)
        probs_used = keep.sems("probs_used", PROB_SLOTS)
        out_copied = keep.sems("out_copied", OUT_SLOTS)
        out_stored = keep.sems("out_stored", OUT_SLOTS)
        waited_pe, waited_dve, waited_sp = keep.sem("waited_tensor"), keep.sem("waited_vector"), keep.sem("waited_sync")
        MAX_STEPS = 5
        CONSTS = 16 * (3 + 4 * HG)
        exp_value = lambda it, n: it * (TILES // SCORE_SLOTS) + n // SCORE_SLOTS + 1
        used_value = lambda it, n: it * (TILES // PROB_SLOTS) + n // PROB_SLOTS + 1
        strip_value = lambda it, x: it * (NSTRIPS // STRIP_SLOTS) + x // STRIP_SLOTS + 1
        out_value = lambda it, gn: it * (NG // OUT_SLOTS) + gn // OUT_SLOTS + 1

        block = ctx.enter_context(nc.Block())

        @block.sync
        def _(sp):
            def load_stack(it, u, c):
                cols = slice(c * CH, (c + 1) * CH)
                for r, (i, j) in enumerate(PAIRS):
                    for stack, src, part in ((q_stack, scr["q"], i), (k_stack, scr["k"], j)):
                        rows = src[part, bass.ds(it * (HG * D), HG * D), cols].rearrange("(j d) t -> d j t", d=D)
                        sp.dma_start(stack[u][r * D:(r + 1) * D, :, cols], rows).then_inc(stack_in[u][c], 16)
                sp.dma_start(k_stack[u][ALIBI_ROW:MAX_ROW, :, cols], io["alibi"][:, bass.ds(it * HG, HG), cols]).then_inc(stack_in[u][c], 16)

            def load_v(it, u):
                sp.dma_start(v_ext[u][:], scr["v"][bass.ds(it, 1)].rearrange("a p k e -> (a p) k e")).then_inc(v_in[u], 16)

            def load_max(it, u):
                sp.wait_ge(max_copied, it + 1)
                for s in range(PARTS):
                    sp.dma_start(q_stack[u][MAX_ROW + s:MAX_ROW + s + 1].rearrange("a j (t x) -> a (j t) x", x=P),
                                 max_t[:, s, :]).then_inc(max_in, 16)

            def group(it, u, more, beside):
                for gn, g in enumerate(ORDER):
                    if more:
                        n = LAST_TILE[g]
                        sp.wait_ge(exp_done[n % SCORE_SLOTS], exp_value(it, n) + 1)
                        sp.sem_inc(waited_sp, 1)
                        load_stack(it + 2, u, g)
                    if g == 1 and beside:
                        load_max(it + 1, 1 - u)
                    slot = gn % OUT_SLOTS
                    sp.wait_ge(out_copied[slot], out_value(it, gn) + 1)
                    sp.sem_inc(waited_sp, 1)
                    sp.dma_start(scr["out"][bass.ds(it * P, P), g * CH:(g + 1) * CH], out_sb[slot][:]).then_inc(out_stored[slot], 16)
                if more:
                    load_v(it + 2, u)

            for slot in range(OUT_SLOTS):
                sp.sem_inc(out_stored[slot], 16)
            sp.sem_inc(max_in, 16 * PARTS)
            sp.dma_start(mask[:], io["mask"]).then_inc(const_in, 16)
            sp.dma_start(tri[:], io["tri"]).then_inc(const_in, 16)
            sp.dma_start(ident[:], io["ident"]).then_inc(const_in, 16)
            for u in range(2):
                for j in range(HG):
                    sp.dma_start(q_stack[u][ALIBI_ROW:MAX_ROW, j, :], io["fixed_rows"][0:ALIBI_ROWS]).then_inc(const_in, 16)
                    sp.dma_start(k_stack[u][MAX_ROW:ROWS, j, :], io["fixed_rows"][ALIBI_ROWS:]).then_inc(const_in, 16)
            for u in range(2):
                for c in range(NG):
                    load_stack(u, u, c)
                load_v(u, u)
            load_max(0, 0)
            with sp.Fori(0, (ITERS - 2) // 2) as pair:
                group(pair * 2, 0, True, True)
                group(pair * 2 + 1, 1, True, True)
            group(ITERS - 2, 0, False, True)
            group(ITERS - 1, 1, False, False)
            for slot in range(OUT_SLOTS):
                sp.wait_ge(out_stored[slot], 16 * (ITERS * NG // OUT_SLOTS + 1))

        @block.tensor
        def _(pe):
            def wait_stack(k, u):
                for c in range(NG):
                    pe.wait_ge(stack_in[u][c], k * (16 * STACK_DMAS) + 16 * STACK_DMAS)

            def strip(it, u, x):
                j, t, s = STRIPS[x]
                width = CH if s < t // BLK else (t % BLK + 1) * P
                pe.wait_ge(strip_free[x % STRIP_SLOTS], strip_value(it, x))
                pe.matmul(p_strip[:, x % STRIP_SLOTS, 0:width], q_stack[u][0:MAX_ROW, j, t * P:(t + 1) * P],
                          k_stack[u][0:MAX_ROW, j, s * CH:s * CH + width], start=True, stop=True).then_inc(strip_ready[x % STRIP_SLOTS], 1)

            def turn_max(it):
                pe.wait_ge(max_step, it * MAX_STEPS + MAX_STEPS)
                pe.sem_inc(waited_pe, 1)
                for s in range(PARTS):
                    mm = pe.transpose(p_max[:, s * P:(s + 1) * P], max_parts[:, s, :], ident[:])
                mm.then_inc(max_turned, 1)

            def scores(it, u, n, tile, g):
                slot = n % SCORE_SLOTS
                pe.wait_ge(exp_done[slot], exp_value(it, n))
                for j, i, q0, cols, at in tile:
                    diagonal = i >= BLK * g
                    mm = pe.matmul(p_score[slot][:, at:at + cols], k_stack[u][0:ROWS, j, i * P:(i + 1) * P],
                                   q_stack[u][0:ROWS, j, g * CH + q0:g * CH + q0 + cols], start=True, stop=not diagonal)
                    if diagonal:
                        mm = pe.matmul(p_score[slot][:, at:at + P], tri[:], ident[:], start=False, stop=True)
                mm.then_inc(score_ready, 1)

            def values(it, u, n0, gn, first, last, step):
                bank = gn % OUT_SLOTS
                pieces = sorted((i, j, q0, cols, at, n0 + s) for s, tile in enumerate(step) for j, i, q0, cols, at in tile)
                if first:
                    pe.wait_ge(out_copied[bank], out_value(it, gn))
                final = {piece[-1]: x for x, piece in enumerate(pieces)}
                waited = n0 - 1
                for x, (i, j, q0, cols, at, n) in enumerate(pieces):
                    if n > waited:
                        pe.wait_ge(exp_done[n % SCORE_SLOTS], exp_value(it, n) + 1)
                        waited = n
                    mm = pe.matmul(p_out[bank][j * OUT_ROWS:(j + 1) * OUT_ROWS, q0:q0 + cols], v_ext[u][:, i, j * OUT_ROWS:(j + 1) * OUT_ROWS],
                                   probs[n % PROB_SLOTS][:, at:at + cols], start=first, stop=last)
                    if final[n] == x:
                        mm.then_inc(probs_used[n % PROB_SLOTS], 1)

            def group(it, k, u, beside):
                pe.wait_ge(max_in, it * (16 * PARTS) + 2 * 16 * PARTS)
                pe.wait_ge(v_in[u], k * 16 + 16)
                n, before = 0, None
                for x, (g, nth, step) in enumerate(STEPS):
                    todo = list(strips_at(x)) if beside else []
                    if beside and x == QUIET_FIRST:
                        wait_stack(k + u, 1 - u)
                        pe.wait_ge(max_copied, it + 1)
                    slots = len(step) + 1
                    share = [todo[len(todo) * s // slots:len(todo) * (s + 1) // slots] for s in range(slots)]
                    for s, tile in enumerate(step):
                        scores(it, u, n + s, tile, g)
                        for y in share[s]:
                            strip(it + 1, 1 - u, y)
                    if before is not None:
                        values(it, u, *before)
                    for y in share[-1]:
                        strip(it + 1, 1 - u, y)
                    before = (n, ORDER.index(g), nth == 0, nth == STEPS_OF[g] - 1, step)
                    n += len(step)
                    if beside and x == TURN_STEP:
                        turn_max(it + 1)
                values(it, u, *before)

            for slot in range(PROB_SLOTS):
                pe.sem_inc(probs_used[slot], 1)
            pe.wait_ge(const_in, CONSTS)
            wait_stack(0, 0)
            for y in range(NSTRIPS):
                strip(0, 0, y)
            turn_max(0)
            with pe.Fori(0, (ITERS - 2) // 2) as pair:
                group(pair * 2, pair, 0, True)
                group(pair * 2 + 1, pair, 1, True)
            group(ITERS - 2, ITERS // 2 - 1, 0, True)
            group(ITERS - 1, ITERS // 2 - 1, 1, False)

        @block.scalar
        def _(act):
            def copy_out(it, g):
                gn, n = ORDER.index(g), LAST_TILE[g]
                slot = gn % OUT_SLOTS
                act.wait_ge(probs_used[n % PROB_SLOTS], used_value(it, n) + 1)
                act.wait_ge(out_stored[slot], (out_value(it, gn)) * 16)
                act.copy(out_sb[slot][:], p_out[slot][:]).then_inc(out_copied[slot], 1)

            for slot in range(SCORE_SLOTS):
                act.sem_inc(exp_done[slot], 1)
            for slot in range(OUT_SLOTS):
                act.sem_inc(out_copied[slot], 1)
            with act.Fori(0, ITERS) as it:
                n = 0
                for g, nth, step in STEPS:
                    for tile in step:
                        cols = sum(piece[3] for piece in tile)
                        act.wait_ge(score_ready, it * TILES + n + 1)
                        act.wait_ge(probs_used[n % PROB_SLOTS], used_value(it, n))
                        act.activation(probs[n % PROB_SLOTS][:, 0:cols], p_score[n % SCORE_SLOTS][:, 0:cols], ACT.Exp).then_inc(exp_done[n % SCORE_SLOTS], 1)
                        n += 1
                    if nth == 1 and g != ORDER[0]:
                        copy_out(it, ORDER[ORDER.index(g) - 1])
                copy_out(it, ORDER[-1])

        @block.gpsimd
        def _(pool):
            pass

        @block.vector
        def _(dve):
            for slot in range(STRIP_SLOTS):
                dve.sem_inc(strip_free[slot], 1)
            dve.memset(strip_max[:], -3.0e38).then_inc(strip_max_set, 1)
            dve.wait_ge(strip_max_set, 1)
            dve.wait_ge(const_in, CONSTS)
            with dve.Fori(0, ITERS) as it:
                diagonals = []
                for x, (j, t, s) in enumerate(STRIPS):
                    slot = x % STRIP_SLOTS
                    dve.wait_ge(strip_ready[slot], strip_value(it, x))
                    dst = strip_max[:, j * NT + t, s:s + 1]
                    if s < t // BLK:
                        dve.tensor_reduce(dst, p_strip[:, slot, :], AX.X, ALU.max).then_inc(strip_free[slot], 1)
                        continue
                    width = (t % BLK + 1) * P
                    if len(diagonals) >= 2:
                        y = diagonals[-2]
                        dve.wait_ge(strip_free[y % STRIP_SLOTS], strip_value(it, y) + 1)
                    dve.sem_inc(waited_dve, 1)
                    dve.tensor_tensor_reduce(unused[len(diagonals) % 2][:, 0:width], p_strip[:, slot, 0:width], mask[:, CH - width:],
                                             1.0, -3.0e38, ALU.add, ALU.max, dst).then_inc(strip_free[slot], 1)
                    diagonals.append(x)
                for slot in range(STRIP_SLOTS):
                    dve.wait_ge(strip_free[slot], strip_value(it, NSTRIPS - STRIP_SLOTS + slot) + 1)
                done = lambda k: it * MAX_STEPS + k
                dve.tensor_reduce(neg_max[:], strip_max[:], AX.X, ALU.max, negate=True).then_inc(max_step, 1)
                dve.wait_ge(max_step, done(1))
                dve.tensor_copy(max_parts[:, 0], neg_max[:]).then_inc(max_step, 1)
                dve.wait_ge(max_step, done(2))
                dve.tensor_tensor(max_rest[:], neg_max[:], max_parts[:, 0], ALU.subtract).then_inc(max_step, 1)
                dve.wait_ge(max_step, done(3))
                dve.tensor_copy(max_parts[:, 1], max_rest[:]).then_inc(max_step, 1)
                dve.wait_ge(max_step, done(4))
                dve.tensor_tensor(max_parts[:, 2], max_rest[:], max_parts[:, 1], ALU.subtract).then_inc(max_step, 1)
                dve.wait_ge(max_in, it * (16 * PARTS) + 16 * PARTS)
                dve.wait_ge(max_turned, it + 1)
                dve.tensor_copy(max_t[:].rearrange("p s x -> p (s x)"), p_max).then_inc(max_copied, 1)


def build_finish(nc, keep, io, scr, w_ternary):
    with ExitStack() as ctx:
        m = Work(nc, ctx)
        w = m.sb("w_proj", [P, KC, C])
        b_proj = m.sb("b_proj", [P, C])
        ident = m.sb("ident_f", [P, P])
        eps = m.sb("eps", [P, 1])
        num = [m.sb(f"num{u}", [P, KC, CH]) for u in range(2)]
        den = [m.sb(f"den{u}", [P, KC, CH]) for u in range(2)]
        x = [m.sb(f"x{u}", [P, BLK, C]) for u in range(2)]
        xb = [m.sb(f"x_bias{u}", [P, BLK, C]) for u in range(2)]
        den_inv = m.sb("den_inv", [P, KC, CH])
        y_t = [m.sb(f"y_t{u}", [P, KC, CH]) for u in range(2)]
        pre = [[m.sb(f"pre{k}_{u}", [P, BLK, C]) for u in range(2)] for k in range(2)]
        stats = [m.sb(f"stats{k}", [P, BLK, 6]) for k in range(2)]
        mv = [m.sb(f"mean_var{k}", [P, BLK, 2]) for k in range(2)]
        dev = [m.sb(f"dev{k}", [P, BLK]) for k in range(2)]
        inv = [m.sb(f"inv{k}", [P, BLK]) for k in range(2)]
        normed = [[m.sb(f"normed{k}_{u}", [P, BLK, C]) for u in range(2)] for k in range(2)]
        h_t = m.sb("h_t", [P, 2, 2, KC, P])
        p_y = [m.psum(f"p_y{h}", [P, 2, C]) for h in range(2)]
        p_t = [m.psum(f"p_t{h}", [P, 2, KC, P]) for h in range(2)]
        p_f = [m.psum(f"p_f{h}", [P, 2, C]) for h in range(2)]

        w_in, eps_set = keep.sem("w_proj_loaded"), keep.sem("eps_set")
        LOADS = 2 * KC + 1
        chunk_in = keep.sems("chunk_loaded", 2)
        xb_ready = keep.sem("x_bias_ready")
        inv_ready, y_ready = keep.sem("den_inv_ready"), keep.sem("y_ready")
        sum_ready = [keep.sems(f"sum{k}_ready", 2) for k in range(2)]
        pre_ready = [keep.sems(f"pre{k}_ready", 2) for k in range(2)]
        stats_ready, mv_ready = keep.sems("stats_ready", 2), keep.sems("mean_var_ready", 2)
        dev_ready, dev_inv_ready = keep.sems("dev_ready", 2), keep.sems("dev_inv_ready", 2)
        normed_ready = [keep.sems(f"normed{k}_ready", 2) for k in range(2)]
        turned, turned_copied = keep.sems("turned", 2), keep.sems("turned_copied", 2)
        result_stored = keep.sems("result_stored", 2)
        waited = keep.sem("waited_for_stats")

        block = ctx.enter_context(nc.Block())
        heads = scr["out"].rearrange("(q r) t -> q r t", r=OUT_ROWS)
        HC = P // D

        @block.sync
        def _(sp):
            sp.dma_start(w[:], io["w_proj"].rearrange("(k p) n -> p k n", p=P)).then_inc(w_in, 16)
            sp.dma_start(b_proj[:], row_to_all(io["b_proj"], C)).then_inc(w_in, 16)
            sp.dma_start(ident[:], io["ident_f"]).then_inc(w_in, 16)
            with sp.Fori(0, B) as b:
                for c in range(NG):
                    u = c % 2
                    sp.wait_ge(y_ready, b * NG + c + 1)
                    sp.wait_ge(xb_ready, b * NG + c + 1)
                    for k in range(KC):
                        rows = heads[bass.ds(b * H + k * HC, HC), :, c * CH:(c + 1) * CH]
                        sp.dma_start(num[u][:, k], rows[:, 0:D]).then_inc(chunk_in[u], 16)
                        sp.dma_start(den[u][:, k], rows[:, D:2 * D]).then_inc(chunk_in[u], 16)
                    sp.dma_start(x[u][:], io["x"][bass.ds(b * T + c * CH, CH)].rearrange("(a p) n -> p a n", p=P)).then_inc(chunk_in[u], 16)

        @block.gpsimd
        def _(pool):
            pool.sem_inc(xb_ready, 2)
            pool.wait_ge(w_in, 48)
            with pool.Fori(0, B) as b:
                for c in range(NG):
                    u = c % 2
                    pool.wait_ge(chunk_in[u], b * (16 * LOADS * NG // 2) + 16 * LOADS * (c // 2 + 1))
                    pool.wait_ge(pre_ready[0][1], b * NG + c + 1)
                    for a in range(BLK):
                        add = pool.tensor_tensor(xb[u][:, a], x[u][:, a], b_proj[:], ALU.add)
                    add.then_inc(xb_ready, 1)

        @block.tensor
        def _(pe):
            def linear(k, b, c, source, weights, half):
                for a in range(2):
                    for i in range(KC):
                        mm = pe.matmul((p_y, p_f)[k][half][:, a], source(a, i), weights[:, i], start=(i == 0), stop=(i == KC - 1))
                mm.then_inc(sum_ready[k][half], 1)

            pe.wait_ge(w_in, 48)
            with pe.Fori(0, B) as b:
                for step in range(NG + 2):
                    if 2 <= step:
                        c = step - 2
                        u, n = c % 2, b * NG + c
                        for half in range(2):
                            pe.wait_ge(normed_ready[0][half], n * 2 + 2)
                            pe.wait_ge(turned_copied[half], n + 1)
                            for a in range(2):
                                for k in range(KC):
                                    mm = pe.transpose(p_t[half][:, a, k], normed[0][u][:, 2 * half + a, k * P:(k + 1) * P], ident[:])
                            mm.then_inc(turned[half], 1)
                    if 1 <= step <= NG:
                        c = step - 1
                        u, n = c % 2, b * NG + c
                        pe.wait_ge(y_ready, n + 3)
                        for half in range(2):
                            pe.wait_ge(pre_ready[0][half], n + 1 + half)
                            linear(0, b, c, lambda a, i: y_t[u][:, i, (2 * half + a) * P:(2 * half + a + 1) * P], w, half)
                    if 2 <= step:
                        c = step - 2
                        n = b * NG + c
                        for half in range(2):
                            pe.wait_ge(turned_copied[half], n + 2)
                            pe.wait_ge(pre_ready[1][half], n + 1)
                            linear(1, b, c, lambda a, i: h_t[:, half, a, i], w_ternary, half)

        @block.scalar
        def _(act):
            def deviation(k, n):
                act.wait_ge(mv_ready[k], n * BLK + BLK)
                act.wait_ge(dev_inv_ready[k], n + 1)
                act.activation(dev[k][:], mv[k][:, :, 1], ACT.Sqrt, bias=eps[:, 0:1]).then_inc(dev_ready[k], 1)

            for half in range(2):
                act.sem_inc(turned_copied[half], 1)
            for u in range(2):
                act.sem_inc(result_stored[u], 16)
            act.wait_ge(eps_set, 1)
            with act.Fori(0, B) as b:
                for step in range(NG + 2):
                    if 2 <= step:
                        n = b * NG + step - 2
                        for half in range(2):
                            act.wait_ge(pre_ready[1][half], n + 1)
                            act.wait_ge(turned[half], n + 1)
                            act.copy(h_t[:, half], p_t[half][:]).then_inc(turned_copied[half], 1)
                    if 1 <= step <= NG:
                        deviation(0, b * NG + step - 1)
                    if 2 <= step:
                        c = step - 2
                        u, n = c % 2, b * NG + c
                        deviation(1, n)
                        for half in range(2):
                            act.wait_ge(normed_ready[1][half], n * 2 + 2)
                        act.dma_start(io["out"][bass.ds(b * T + c * CH, CH)].rearrange("(a p) n -> p a n", p=P),
                                      normed[1][u][:]).then_inc(result_stored[u], 16)
            for u in range(2):
                act.wait_ge(result_stored[u], 16 * (B * NG // 2 + 1))

        @block.vector
        def _(dve):
            def normalise_attention(b, c):
                u, n = c % 2, b * NG + c
                dve.wait_ge(chunk_in[u], b * (16 * LOADS * NG // 2) + 16 * LOADS * (c // 2 + 1))
                dve.wait_ge(y_ready, n + 2)
                dve.reciprocal(den_inv[:], den[u][:]).then_inc(inv_ready, 1)
                dve.wait_ge(inv_ready, n + 1)
                dve.tensor_tensor(y_t[u][:], num[u][:], den_inv[:], ALU.mult).then_inc(y_ready, 1)

            def add_and_measure(k, b, c):
                u, n = c % 2, b * NG + c
                bank, other = ((p_y, xb), (p_f, normed[0]))[k]
                given = 2 if k == 0 else 1
                for half in range(2):
                    if k == 0 and half == 0:
                        dve.wait_ge(xb_ready, n + 3)
                    dve.wait_ge(sum_ready[k][half], n + 1)
                    dve.tensor_tensor(pre[k][u][:, 2 * half:2 * half + 2], bank[half][:], other[u][:, 2 * half:2 * half + 2],
                                      ALU.add).then_inc(pre_ready[k][half], 1)
                for a in range(BLK):
                    given = 1 + (1 if k == 0 and a // 2 == 1 else 0)
                    dve.wait_ge(pre_ready[k][a // 2], n + given + 1)
                    dve.bn_stats(stats[k][:, a], pre[k][u][:, a]).then_inc(stats_ready[k], 1)
                for a in range(BLK):
                    dve.wait_ge(stats_ready[k], n * BLK + a + 1)
                    dve.sem_inc(waited, 1)
                    dve.bn_aggr(mv[k][:, a], stats[k][:, a]).then_inc(mv_ready[k], 1)

            def normalise(k, b, c):
                u, n = c % 2, b * NG + c
                dve.wait_ge(dev_ready[k], n + 1)
                dve.reciprocal(inv[k][:], dev[k][:]).then_inc(dev_inv_ready[k], 1)
                if k == 1:
                    dve.wait_ge(result_stored[u], b * (16 * NG // 2) + 16 * (c // 2 + 1))
                dve.wait_ge(dev_inv_ready[k], n + 2)
                for a in range(BLK):
                    dve.tensor_scalar(normed[k][u][:, a], pre[k][u][:, a], mv[k][:, a, 0:1], inv[k][:, a:a + 1],
                                      ALU.subtract, ALU.mult).then_inc(normed_ready[k][a // 2], 1)

            dve.sem_inc(y_ready, 2)
            dve.sem_inc(pre_ready[0][0], 1)
            dve.sem_inc(pre_ready[0][1], 2)
            for k in range(2):
                dve.sem_inc(pre_ready[1][k], 1)
                dve.sem_inc(dev_inv_ready[k], 1)
            dve.memset(eps[:], EPS).then_inc(eps_set, 1)
            with dve.Fori(0, B) as b:
                for step in range(NG + 2):
                    if step < NG:
                        normalise_attention(b, step)
                    if 1 <= step <= NG:
                        add_and_measure(0, b, step - 1)
                    if 2 <= step:
                        add_and_measure(1, b, step - 2)
                    if 1 <= step <= NG:
                        normalise(0, b, step - 1)
                    if 2 <= step:
                        normalise(1, b, step - 2)


def build(nc, io):
    scr = {
        "q": nc.dram_tensor("q_parts", (PARTS, B * C, T), BF16, kind="Internal").ap(),
        "k": nc.dram_tensor("k_parts", (PARTS, B * C, T), BF16, kind="Internal").ap(),
        "v": nc.dram_tensor("v_extended", (ITERS, P, NT, VW), F32, kind="Internal").ap(),
        "out": nc.dram_tensor("attention_sums", (ITERS * P, T), F32, kind="Internal").ap(),
    }
    with ExitStack() as ctx:
        keep = Work(nc, ctx)
        w_ternary = keep.sb("w_ternary", [P, KC, C])
        build_project(nc, keep, io, scr, w_ternary)
        build_attend(nc, keep, io, scr)
        build_finish(nc, keep, io, scr, w_ternary)


def kernel(L0_attn_x, L0_attn_W_attn, L0_attn_b_attn, L0_attn_W_proj, L0_attn_b_proj, L0_attn_temperature, L0_ffn_weight):
    import ml_dtypes
    import concourse.bacc as bacc
    from concourse.bass_utils import run_bass_kernel_spmd

    x = np.ascontiguousarray(L0_attn_x).reshape(B * T, C)
    alibi, fixed_rows, tri, mask, ident = constants(np.dtype(ml_dtypes.bfloat16))
    arrays = {
        "x": x,
        "x_t": np.ascontiguousarray(x.T),
        "w_attn": np.ascontiguousarray(L0_attn_W_attn),
        "b_qk": np.ascontiguousarray(np.asarray(L0_attn_b_attn)[:2 * C].reshape(2 * KC, P).T),
        "b_v": np.ascontiguousarray(np.asarray(L0_attn_b_attn)[2 * C:]),
        "w_proj": np.ascontiguousarray(L0_attn_W_proj),
        "b_proj": np.ascontiguousarray(L0_attn_b_proj),
        "temperature": np.ascontiguousarray(L0_attn_temperature),
        "w_ffn_t": np.ascontiguousarray(np.asarray(L0_ffn_weight).T),
        "alibi": alibi,
        "fixed_rows": fixed_rows,
        "tri": tri,
        "mask": mask,
        "ident": ident.astype(tri.dtype),
        "ident_f": ident,
    }
    nc = bacc.Bacc("TRN2", target_bir_lowering=False, num_devices=1)
    io = {name: nc.dram_tensor(f"in_{name}", a.shape, mybir.dt.from_np(a.dtype), kind="ExternalInput").ap() for name, a in arrays.items()}
    io["out"] = nc.dram_tensor("out", (B * T, C), F32, kind="ExternalOutput").ap()
    build(nc, io)
    r = run_bass_kernel_spmd(nc, [{f"in_{name}": a for name, a in arrays.items()}], core_ids=[0])
    return r.results[0]["out"].reshape(B, T, C)
```

```python
from contextlib import ExitStack

import numpy as np
import concourse.bass as bass
from concourse import mybir

F32 = mybir.dt.float32
BF16 = mybir.dt.bfloat16
ALU = mybir.AluOpType
ACT = mybir.ActivationFunctionType
AX = mybir.AxisListType

P = 128
B, T, C, H = 4, 2048, 256, 16
D = C // H
HG = 4
ITERS = B * H // HG
CH = 512
NG = T // CH
BLK = CH // P
NT = T // P
KC = C // P
PARTS = 3
Q_STACK, K_STACK = (0, 1, 1, 2, 0, 0), (1, 0, 1, 0, 0, 2)
PAIRS = list(zip(Q_STACK, K_STACK))
Q_STORED, K_STORED = (0, 1, 2), (1, 0, 2)
Q_RUNS = ((0, 0, 2), (2, 1, 2), (4, 0, 1), (5, 0, 1))
K_RUNS = ((0, 0, 2), (2, 0, 2), (4, 1, 2))
for stack, order, runs in ((Q_STACK, Q_STORED, Q_RUNS), (K_STACK, K_STORED, K_RUNS)):
    assert all(stack[r + i] == order[s + i] for r, s, n in runs for i in range(n)) and sum(n for *_, n in runs) == len(PAIRS)
assert len(set(PAIRS)) == 6 and all(i + j <= 2 for i, j in PAIRS)
STACK_DMAS = len(Q_RUNS) + len(K_RUNS) + 1
ALIBI_ROW = len(PAIRS) * D
ALIBI_ROWS = PARTS * NG
MAX_ROW = ALIBI_ROW + ALIBI_ROWS
ROWS = MAX_ROW + PARTS
NEG = -1.0e30
EPS = 1e-5
OUT_ROWS = 2 * D
VW = HG * OUT_ROWS


def constants(bf16):
    start = 2.0 ** (-2.0 ** (-(np.log2(H) - 3)))
    slopes = np.array([start * start ** i for i in range(H)]).astype(np.float32)
    centre = np.arange(NG, dtype=np.float32) * CH + CH // 2
    rest = (slopes[None, :, None] * (np.arange(T, dtype=np.float32)[None, None, :] - centre[:, None, None])).astype(np.float32)
    alibi = []
    for _ in range(PARTS):
        alibi.append(rest.astype(bf16))
        rest = rest - alibi[-1].astype(np.float32)
    in_chunk = np.arange(T)[None, :] // CH == np.arange(NG)[:, None]
    fixed_rows = np.concatenate([in_chunk] * PARTS + [np.ones((PARTS, T), bool)]).astype(bf16)
    mask = np.zeros((P, CH), np.float32)
    mask[:, CH - P:] = np.triu(np.full((P, P), NEG, np.float32), 1)
    alibi = np.tile(np.concatenate(alibi), (1, B, 1))
    return alibi, fixed_rows, mask[:, CH - P:].astype(bf16), mask, np.eye(P, dtype=np.float32)


def pass2_tiles(g):
    steps = []
    for i in range(BLK * g):
        steps.append([[(j, i, 0, CH, (j % 2) * CH) for j in (2 * s, 2 * s + 1)] for s in range(2)])
    d = BLK * g
    steps.append([[(j, d, 0, CH, (j % 2) * CH) for j in (2 * s, 2 * s + 1)] for s in range(2)])
    steps.append([[piece for j in (2 * s, 2 * s + 1) for piece in
                   ((j, d + 1, P, CH - P, (j % 2) * CH), (j, d + 3, 3 * P, P, (j % 2) * CH + CH - P))]
                  for s in range(2)])
    steps.append([[(j, d + 2, 2 * P, 2 * P, j * 2 * P) for j in range(HG)]])
    return steps


ORDER = list(reversed(range(NG)))
STEPS = [(g, n, step) for g in ORDER for n, step in enumerate(pass2_tiles(g))]
TILES = sum(len(step) for _, _, step in STEPS)
STEPS_OF = {g: len(pass2_tiles(g)) for g in ORDER}
LAST_TILE = {g: sum(len(step) for gg, _, step in STEPS if ORDER.index(gg) <= ORDER.index(g)) - 1 for g in ORDER}

STRIPS = [(g, s, j, BLK * g + t) for g in ORDER for s in reversed(range(g + 1)) for j in range(HG) for t in range(BLK)]


def strip_width(g, s, t):
    return CH if s < g else (t % BLK + 1) * P


def pass1_items():
    items = []
    for x, strip in enumerate(STRIPS):
        items.append(("strip", x))
        before = x - TURN_AFTER
        if before >= 0 and strip[0] != STRIPS[0][0] and STRIPS[before][0] != STRIPS[before + 1][0]:
            items.append(("turn", STRIPS[before][0]))
    return items


TURN_AFTER = 4
FIRST_ITEMS = pass1_items()
LAST_ITEMS = [("turn", 0)]
ITEMS = FIRST_ITEMS[:TURN_AFTER] + LAST_ITEMS + FIRST_ITEMS[TURN_AFTER:]

SCORE_SLOTS, PROB_SLOTS, STRIP_SLOTS = 2, 4, 3
OUT_BUFS = 2
BESIDE_PV, BESIDE_COLUMN = 900, 0.417


def place_items(items):
    now, freed, taken, placed = 0.0, [], 0, []

    def fill():
        nonlocal now, taken
        n = 0
        while taken < len(items) and (taken < STRIP_SLOTS or freed[taken - STRIP_SLOTS] + 60 <= now):
            kind, x = items[taken]
            width = P if kind == "turn" else strip_width(STRIPS[x][0], STRIPS[x][1], STRIPS[x][3])
            now += 3 + BESIDE_COLUMN * width
            start = max(now + 60, freed[-1] if freed else 0)
            freed.append(start + 85 + 1.042 * width + (900 if kind == "turn" else 0))
            taken += 1
            n += 1
        placed.append(n)

    for k, (g, nth, step) in enumerate(STEPS):
        for tile in step:
            for j, i, q0, cols, at in tile:
                now += 3 + BESIDE_COLUMN * (cols + (P if i >= BLK * g else 0))
                fill()
        now += BESIDE_PV * sum(piece[3] for tile in step for piece in tile) / (HG * CH)
        fill()
    placed[-1] += len(items) - taken
    return placed


class Work:

    def __init__(self, nc, ctx):
        self.nc, self.ctx = nc, ctx

    def sb(self, name, shape, dtype=F32):
        return self.ctx.enter_context(self.nc.sbuf_tensor(name, shape, dtype))

    def psum(self, name, shape, dtype=F32):
        return self.ctx.enter_context(self.nc.psum_tensor(name, shape, dtype))

    def sem(self, name):
        return self.ctx.enter_context(self.nc.semaphore(name))

    def sems(self, name, n):
        return [self.sem(f"{name}{i}") for i in range(n)]


def row_to_all(vector, n):
    return vector.rearrange("(a n) -> a n", a=1).broadcast_to([P, n])


def build_project(nc, keep, io, scr, w_ternary, block, p_score, p_strip, p_out, beside):
    with ExitStack() as ctx:
        m = Work(nc, ctx)
        w = m.sb("w_attn", [P, KC, 3 * C])
        b_qk = m.sb("b_qk", [P, 2 * KC])
        b_v = m.sb("b_v", [P, C])
        temp = m.sb("temp", [P, 1])
        temp_inv = m.sb("temp_inv", [P, 1])
        scale = m.sb("scale", [P, 1])
        b_q = m.sb("b_q_scaled", [P, KC])
        w_ffn = m.sb("w_ffn", [P, KC, C])
        ones = m.sb("ones", [P, P])
        abs_sum = m.sb("abs_sum", [P, 1])
        w_scale = m.sb("w_scale", [P, 1])
        half = m.sb("half_scale", [P, 2])
        below = m.sb("below", [P, KC, C])
        above = m.sb("above", [P, KC, C])
        xt = m.sb("xt", [P, 2, KC, CH])
        full = m.sb("full", [P, 4, CH])
        rest = m.sb("rest", [P, 2, CH])
        parts = m.sb("parts", [P, 2, PARTS, 4, CH], BF16)
        vx = m.sb("vx", [P, 2, HG, BLK, VW])
        p_qk = [p_score[o // 2][:, o % 2 * CH:(o % 2 + 1) * CH] for o in range(4)]
        p_v = [p_strip[:, h].rearrange("p (a n) -> p a n", n=C) for h in range(2)]
        p_sum = p_out[:, 0:1]

        w_in, ffn_in = keep.sem("w_loaded"), keep.sem("ffn_weight_loaded")
        xt_in = keep.sems("xt_loaded", 2)
        ones_ready = keep.sem("ones_ready")
        abs_ready, total_ready = keep.sem("abs_sum_ready"), keep.sem("total_ready")
        prep = keep.sem("preparation_steps")
        qk_ready, qk_free = keep.sems("qk_sums_ready", 4), keep.sems("qk_bank_free", 4)
        v_ready, v_free = keep.sems("v_sums_ready", 2), keep.sems("v_bank_free", 2)
        full_ready = keep.sem("full_ready")
        rest_ready, part2_ready = keep.sem("rest_ready"), keep.sem("part2_ready")
        parts_ready = keep.sems("parts_ready", 4)
        stored = keep.sems("scratch_stored", 2)
        STORES = 5
        place = lambda o, part: (Q_STORED if o < KC else K_STORED).index(part)

        def load_xt(sp, n, u):
            sp.dma_start(xt[:, u], io["x_t"].rearrange("(k p) t -> p k t", p=P)[:, :, bass.ds(n * CH, CH)]).then_inc(xt_in[u], 16)

        @block.sync
        def _(sp):
            for u in range(2):
                sp.sem_inc(stored[u], 16 * STORES)
            sp.dma_start(w[:], io["w_attn"].rearrange("(k p) n -> p k n", p=P)).then_inc(w_in, 16)
            for u in range(2):
                load_xt(sp, u, u)
            sp.dma_start(b_qk[:], io["b_qk"]).then_inc(w_in, 16)
            sp.dma_start(b_v[:], row_to_all(io["b_v"], C)).then_inc(w_in, 16)
            sp.dma_start(temp[:], row_to_all(io["temperature"], 1)).then_inc(w_in, 16)
            sp.dma_start(w_ffn[:], io["w_ffn_t"].rearrange("(k p) n -> p k n", p=P)).then_inc(ffn_in, 16)
            beside(sp, None)

            def batch(b, last):
                for c in range(NG):
                    u = c % 2
                    for o in range(4):
                        sp.wait_ge(parts_ready[o], b * NG + c + 1 + 1)
                        half = slice((o % KC) * D // KC, (o % KC + 1) * D // KC)
                        dst = (scr["q"] if o < KC else scr["k"])[bass.ds(b, 1), :, half, :, c * CH:(c + 1) * CH]
                        sp.dma_start(dst.rearrange("a s d h t -> (a d h) s t"), parts[:, u, :, o, :]).then_inc(stored[u], 16)
                    for h in range(2):
                        sp.wait_ge(v_free[h], b * NG + c + 1 + 1)
                    dst = scr["v"][bass.ds(b * HG, HG), :, c * BLK:(c + 1) * BLK, :].rearrange("g p a e -> p g (a e)")
                    sp.dma_start(dst, vx[:, u].rearrange("p g a e -> p g (a e)")).then_inc(stored[u], 16)
                    if not (last and c >= NG - 2):
                        load_xt(sp, b * NG + c + 2, u)
                    if last:
                        beside(sp, c)

            with sp.Fori(0, B - 1) as b:
                batch(b, False)
            for u in range(2):
                sp.wait_ge(stored[u], 16 * STORES * ((B - 1) * NG // 2 + 1))
            batch(B - 1, True)
            for u in range(2):
                sp.wait_ge(stored[u], 16 * STORES * (B * NG // 2 + 1))

        @block.tensor
        def _(pe):
            pe.wait_ge(w_in, 64)
            pe.wait_ge(ones_ready, 1)
            pe.wait_ge(abs_ready, 1)
            pe.matmul(p_sum, ones[:], abs_sum[:], start=True, stop=True).then_inc(total_ready, 1)
            with pe.Fori(0, B) as b:
                for c in range(NG):
                    u = c % 2
                    pe.wait_ge(xt_in[u], b * (16 * NG // 2) + 16 * (c // 2 + 1))
                    for o in range(4):
                        pe.wait_ge(qk_free[o], b * NG + c + 1)
                        for k in range(KC):
                            mm = pe.matmul(p_qk[o], w[:, k, o * P:(o + 1) * P], xt[:, u, k, :], start=(k == 0), stop=(k == KC - 1))
                        mm.then_inc(qk_ready[o], 1)
                    for a in range(BLK):
                        if a % 2 == 0:
                            pe.wait_ge(v_free[a // 2], b * NG + c + 1)
                        for k in range(KC):
                            mm = pe.matmul(p_v[a // 2][:, a % 2], xt[:, u, k, a * P:(a + 1) * P], w[:, k, 2 * C:3 * C],
                                           start=(k == 0), stop=(k == KC - 1))
                        if a % 2 == 1:
                            mm.then_inc(v_ready[a // 2], 1)

        @block.scalar
        def _(act):
            for o in range(4):
                act.sem_inc(qk_free[o], 1)
            act.wait_ge(w_in, 64)
            act.wait_ge(prep, 3)
            with act.Fori(0, B) as b:
                for c in range(NG):
                    u = c % 2
                    act.wait_ge(stored[u], b * (16 * STORES * NG // 2) + 16 * STORES * (c // 2 + 1))
                    for o in range(4):
                        act.wait_ge(qk_ready[o], b * NG + c + 1)
                        act.wait_ge(parts_ready[o], b * NG + c + 1)
                        sc, bi = (scale[:, 0:1], b_q[:, o:o + 1]) if o < KC else (1.0, b_qk[:, o:o + 1])
                        act.activation(full[:, o], p_qk[o], ACT.Identity, bias=bi, scale=sc).then_inc(full_ready, 1)
                        act.activation(parts[:, u, place(o, 0), o], p_qk[o], ACT.Identity, bias=bi, scale=sc).then_inc(qk_free[o], 1)

        @block.vector
        def _(dve):
            for o in range(4):
                dve.sem_inc(parts_ready[o], 1)
            for h in range(2):
                dve.sem_inc(v_free[h], 1)
            dve.memset(ones[:], 1.0).then_inc(ones_ready, 1)
            dve.memset(vx[:], 1.0).then_inc(ones_ready, 1)
            dve.wait_ge(w_in, 64)
            dve.reciprocal(temp_inv[:], temp[:]).then_inc(prep, 1)
            dve.wait_ge(prep, 1)
            dve.tensor_scalar(scale[:], temp_inv[:], D ** -0.5, None, ALU.mult).then_inc(prep, 1)
            dve.wait_ge(prep, 2)
            dve.tensor_scalar(b_q[:], b_qk[:, 0:KC], scale[:, 0:1], None, ALU.mult).then_inc(prep, 1)
            dve.wait_ge(ffn_in, 16)
            dve.tensor_reduce(abs_sum[:], w_ffn[:], AX.XY, ALU.add, apply_absolute_value=True).then_inc(abs_ready, 1)
            dve.wait_ge(total_ready, 1)
            dve.tensor_scalar(w_scale[:], p_sum, 1.0 / (C * C), EPS, ALU.mult, ALU.max).then_inc(prep, 1)
            dve.wait_ge(prep, 4)
            dve.tensor_scalar(half[:, 0:1], w_scale[:], 0.5, None, ALU.mult).then_inc(prep, 1)
            dve.tensor_scalar(half[:, 1:2], w_scale[:], -0.5, None, ALU.mult).then_inc(prep, 1)
            dve.wait_ge(prep, 6)
            dve.tensor_scalar(above[:], w_ffn[:], half[:, 0:1], w_scale[:, 0:1], ALU.is_gt, ALU.mult).then_inc(prep, 1)
            dve.tensor_scalar(below[:], w_ffn[:], half[:, 1:2], w_scale[:, 0:1], ALU.is_lt, ALU.mult).then_inc(prep, 1)
            dve.wait_ge(prep, 8)
            dve.tensor_tensor(w_ternary[:], above[:], below[:], ALU.subtract).then_inc(prep, 1)
            dve.wait_ge(ones_ready, 2)
            with dve.Fori(0, B) as b:
                for c in range(NG):
                    u = c % 2
                    for o in range(4):
                        dve.wait_ge(qk_free[o], b * NG + c + 1 + 1)
                        dve.wait_ge(parts_ready[(o + 2) % 4], b * NG + c + 1 + (o >= 2))
                        dve.tensor_tensor(rest[:, o % 2], full[:, o], parts[:, u, place(o, 0), o], ALU.subtract).then_inc(rest_ready, 1)
                        dve.wait_ge(rest_ready, b * (4 * NG) + 4 * c + o + 1)
                        dve.tensor_copy(parts[:, u, place(o, 1), o], rest[:, o % 2]).then_inc(part2_ready, 1)
                        dve.wait_ge(part2_ready, b * (4 * NG) + 4 * c + o + 1)
                        dve.tensor_tensor(parts[:, u, place(o, 2), o], rest[:, o % 2], parts[:, u, place(o, 1), o], ALU.subtract).then_inc(parts_ready[o], 1)
                    dve.wait_ge(stored[u], b * (16 * STORES * NG // 2) + 16 * STORES * (c // 2 + 1))
                    for a in range(BLK):
                        dve.wait_ge(v_ready[a // 2], b * NG + c + 1)
                        dst = vx[:, u, :, a, :].rearrange("p g (j e) -> p g j e", e=OUT_ROWS)[:, :, :, 0:D]
                        add = dve.tensor_tensor(dst, p_v[a // 2][:, a % 2].rearrange("p (g j e) -> p g j e", g=HG, e=D),
                                                b_v[:].rearrange("p (g j e) -> p g j e", g=HG, e=D), ALU.add)
                        if a % 2 == 1:
                            add.then_inc(v_free[a // 2], 1)
        return [(sem, B * NG + 1) for sem in qk_free + v_free] + [(prep, 4)]


def build_attend(nc, keep, io, scr, w_ternary):
    with ExitStack() as ctx:
        m = Work(nc, ctx)
        q_stack = [m.sb(f"q_stack{u}", [P, NG, HG, CH], BF16) for u in range(2)]
        k_stack = [m.sb(f"k_stack{u}", [P, NG, HG, CH], BF16) for u in range(2)]
        v_ext = [m.sb(f"v_ext{u}", [P, NT, VW]) for u in range(2)]
        probs = [m.sb(f"probs{i}", [P, 2 * CH]) for i in range(PROB_SLOTS)]
        out_sb = [m.sb(f"out_sb{i}", [P, CH]) for i in range(OUT_BUFS)]
        mask = m.sb("mask", [P, CH])
        tri = m.sb("tri", [P, P], BF16)
        ident = m.sb("ident", [P, P], BF16)
        unused = [m.sb(f"unused{i}", [P, CH], BF16) for i in range(2)]
        strip_max = m.sb("strip_max", [P, HG, NT, NG])
        neg_max = m.sb("neg_max", [P, HG, BLK])
        max_rest = m.sb("max_rest", [P, HG, BLK])
        max_parts = m.sb("max_parts", [P, PARTS, HG, BLK], BF16)
        max_t = [m.sb(f"max_t{i}", [PARTS * HG * BLK, P], BF16) for i in range(2)]
        den = m.sb("den", [P, HG, T // P])
        den_inv = m.sb("den_inv", [P, HG, T // P])
        p_strip = m.psum("p_strip", [P, STRIP_SLOTS, CH])
        p_score = [m.psum(f"p_score{i}", [P, 2 * CH]) for i in range(SCORE_SLOTS)]
        p_out = m.psum("p_out", [P, CH])
        p_max = [p_strip[0:PARTS * HG * BLK, slot, 0:P // 2].bitcast(BF16) for slot in range(STRIP_SLOTS)]

        const_in = keep.sem("constants_loaded")
        stack_in = [keep.sems(f"stack{u}_columns_loaded", NG) for u in range(2)]
        v_in = keep.sems("v_loaded", 2)
        max_in = keep.sems("max_rows_loaded", NG)
        strip_ready, strip_free = keep.sems("strip_ready", STRIP_SLOTS), keep.sems("strip_bank_free", STRIP_SLOTS)
        max_step = keep.sem("max_steps")
        score_ready = keep.sem("score_ready")
        exp_done = keep.sems("exp_done", SCORE_SLOTS)
        probs_used = keep.sems("probs_used", PROB_SLOTS)
        out_copied = keep.sem("out_copied")
        out_stored = keep.sems("out_stored", OUT_BUFS)
        den_in, den_inverted, inv_stored = keep.sem("den_loaded"), keep.sem("den_inverted"), keep.sem("inv_stored")
        waited_pe, waited_dve, waited_sp, waited_pool = (keep.sem(f"waited_{e}") for e in ("tensor", "vector", "sync", "pool"))
        MAX_STEPS = 5
        CONSTS = 16 * (3 + 4 * HG)
        exp_value = lambda it, n: it * (TILES // SCORE_SLOTS) + n // SCORE_SLOTS + 1
        used_value = lambda it, n: it * (TILES // PROB_SLOTS) + n // PROB_SLOTS + 1

        def item_value(it, x):
            slot = x % STRIP_SLOTS
            uses = lambda items: len(range(slot, len(items), STRIP_SLOTS))
            return x // STRIP_SLOTS + 1 + (0 if it is None else it * uses(ITEMS) + uses(FIRST_ITEMS))

        def turns(it, items):
            for x, (kind, g) in enumerate(items):
                if kind == "turn":
                    yield x, g, ORDER.index(g), (0 if it is None else it if g == 0 else it + 1)

        block = ctx.enter_context(nc.Block())

        def load_stack(sp, it, u, c):
            cols = slice(c * CH, (c + 1) * CH)
            for stack, src, runs in ((q_stack, scr["q"], Q_RUNS), (k_stack, scr["k"], K_RUNS)):
                batch, heads_from = it // (H // HG), it % (H // HG) * HG
                heads = src[bass.ds(batch, 1), :, :, bass.ds(heads_from, HG)].rearrange("a s d j t -> (a s d) j t")
                for r, s, n in runs:
                    sp.dma_start(stack[u][r * D:(r + n) * D, c], heads[s * D:(s + n) * D, :, cols]).then_inc(stack_in[u][c], 16)
            sp.dma_start(k_stack[u][ALIBI_ROW:MAX_ROW, c], io["alibi"][:, bass.ds(it * HG, HG), cols]).then_inc(stack_in[u][c], 16)

        def beside_project(sp, c):
            if c is None:
                sp.dma_start(mask[:], io["mask"]).then_inc(const_in, 16)
                sp.dma_start(tri[:], io["tri"]).then_inc(const_in, 16)
                sp.dma_start(ident[:], io["ident"]).then_inc(const_in, 16)
                for u in range(2):
                    for j in range(HG):
                        sp.dma_start(q_stack[u][ALIBI_ROW:MAX_ROW, :, j], io["fixed_rows"][0:ALIBI_ROWS].rearrange("r (g x) -> r g x", x=CH)).then_inc(const_in, 16)
                        sp.dma_start(k_stack[u][MAX_ROW:ROWS, :, j], io["fixed_rows"][ALIBI_ROWS:].rearrange("r (g x) -> r g x", x=CH)).then_inc(const_in, 16)
            else:
                load_stack(sp, 0, 0, ORDER[c])

        banks_free = build_project(nc, keep, io, scr, w_ternary, block, p_score, p_strip, p_out, beside_project)

        @block.sync
        def _(sp):
            def load_v(it, u):
                sp.dma_start(v_ext[u][:], scr["v"][bass.ds(it, 1)].rearrange("a p k e -> (a p) k e")).then_inc(v_in[u], 16)

            def group(it, u, more):
                for gn, g in enumerate(ORDER):
                    if more:
                        n = LAST_TILE[g]
                        sp.wait_ge(exp_done[n % SCORE_SLOTS], exp_value(it, n) + 1)
                        sp.sem_inc(waited_sp, 1)
                        load_stack(sp, it + 2, u, g)
                    sp.wait_ge(out_copied, it * NG + gn + 2)
                    sp.sem_inc(waited_sp, 1)
                    sp.dma_start(scr["out"][bass.ds(it * P, P), g * CH:(g + 1) * CH], out_sb[gn % OUT_BUFS][:]).then_inc(out_stored[gn % OUT_BUFS], 16)
                if more:
                    load_v(it + 2, u)

            for i in range(OUT_BUFS):
                sp.sem_inc(out_stored[i], 16)
            for c in ORDER:
                load_stack(sp, 1, 1, c)
            for u in range(2):
                load_v(u, u)
            with sp.Fori(0, (ITERS - 2) // 2) as pair:
                group(pair * 2, 0, True)
                group(pair * 2 + 1, 1, True)
            group(ITERS - 2, 0, False)
            group(ITERS - 1, 1, False)

        @block.gpsimd
        def _(pool):
            def load_max(it, items, u):
                for x, g, gn, owner in turns(it, items):
                    pool.wait_ge(strip_free[x % STRIP_SLOTS], item_value(it, x) + 1)
                    pool.sem_inc(waited_pool, 1)
                    half = u if g == 0 else 1 - u
                    for s in range(PARTS):
                        pool.dma_start(q_stack[half][MAX_ROW + s:MAX_ROW + s + 1, g].rearrange("a j (t x) -> a (j t) x", x=P),
                                       max_t[gn % 2][s * HG * BLK:(s + 1) * HG * BLK, :]).then_inc(max_in[gn], 16)

            def load_den(it):
                if not (isinstance(it, int) and it == 0):
                    pool.wait_ge(inv_stored, it * 16)
                for i in range(OUT_BUFS):
                    pool.wait_ge(out_stored[i], it * (16 * NG // OUT_BUFS) + 16 * (NG // OUT_BUFS + 1))
                pool.sem_inc(waited_pool, 1)
                rows = scr["out"][bass.ds(it * P, P)].rearrange("(j r) (p x) -> r p j x", r=OUT_ROWS, p=P)
                pool.dma_start(den[:], rows[D]).then_inc(den_in, 16)

            def store_inverse(it):
                pool.wait_ge(den_inverted, it + 1)
                pool.sem_inc(waited_pool, 1)
                pool.dma_start(scr["inv"][bass.ds(it * HG, HG)].rearrange("j (p x) -> p j x", p=P), den_inv[:]).then_inc(inv_stored, 16)

            load_max(None, FIRST_ITEMS, 1)
            load_max(0, ITEMS, 0)
            load_den(0)
            load_max(1, ITEMS, 1)
            store_inverse(0)
            with pool.Fori(1, (ITERS - 2) // 2) as pair:
                for u in range(2):
                    load_den(pair * 2 + u - 1)
                    load_max(pair * 2 + u, ITEMS, u)
                    store_inverse(pair * 2 + u - 1)
            load_den(ITERS - 3)
            load_max(ITERS - 2, ITEMS, 0)
            store_inverse(ITERS - 3)
            load_max(ITERS - 1, LAST_ITEMS, 1)
            load_den(ITERS - 2)
            store_inverse(ITERS - 2)
            load_den(ITERS - 1)
            store_inverse(ITERS - 1)
            pool.wait_ge(inv_stored, 16 * ITERS)

        @block.tensor
        def _(pe):
            def item(it, items, x, u):
                kind, what = items[x]
                slot = x % STRIP_SLOTS
                if kind == "turn":
                    gn = ORDER.index(what)
                    owner = 0 if it is None else it if what == 0 else it + 1
                    pe.wait_ge(max_step, owner * (NG * MAX_STEPS) + (gn + 1) * MAX_STEPS)
                    pe.wait_ge(strip_free[slot], item_value(it, x))
                    pe.sem_inc(waited_pe, 1)
                    pe.transpose(p_max[slot], max_parts[:].rearrange("p s j t -> p (s j t)"), ident[:]).then_inc(strip_ready[slot], 1)
                    return
                g, s, j, t = STRIPS[what]
                width = strip_width(g, s, t)
                pe.wait_ge(strip_free[slot], item_value(it, x))
                pe.matmul(p_strip[:, slot, 0:width], q_stack[u][0:MAX_ROW, g, j, t % BLK * P:(t % BLK + 1) * P],
                          k_stack[u][0:MAX_ROW, s, j, 0:width], start=True, stop=True).then_inc(strip_ready[slot], 1)

            def scores(it, u, n, tile, g, fill):
                slot = n % SCORE_SLOTS
                pe.wait_ge(exp_done[slot], exp_value(it, n))
                for y, (j, i, q0, cols, at) in enumerate(tile):
                    diagonal = i >= BLK * g
                    mm = pe.matmul(p_score[slot][:, at:at + cols], k_stack[u][0:ROWS, i // BLK, j, i % BLK * P:(i % BLK + 1) * P],
                                   q_stack[u][0:ROWS, g, j, q0:q0 + cols], start=True, stop=not diagonal)
                    if diagonal:
                        mm = pe.matmul(p_score[slot][:, at:at + P], tri[:], ident[:], start=False, stop=True)
                    if y == len(tile) - 1:
                        mm.then_inc(score_ready, 1)
                    fill()

            def values(it, u, n0, gn, first, last, step):
                pieces = sorted((i, j, q0, cols, at, n0 + s) for s, tile in enumerate(step) for j, i, q0, cols, at in tile)
                if first:
                    pe.wait_ge(out_copied, it * NG + gn + 1)
                final = {piece[-1]: x for x, piece in enumerate(pieces)}
                waited = n0 - 1
                for x, (i, j, q0, cols, at, n) in enumerate(pieces):
                    if n > waited:
                        pe.wait_ge(exp_done[n % SCORE_SLOTS], exp_value(it, n) + 1)
                        waited = n
                    mm = pe.matmul(p_out[j * OUT_ROWS:(j + 1) * OUT_ROWS, q0:q0 + cols], v_ext[u][:, i, j * OUT_ROWS:(j + 1) * OUT_ROWS],
                                   probs[n % PROB_SLOTS][:, at:at + cols], start=first, stop=last)
                    if final[n] == x:
                        mm.then_inc(probs_used[n % PROB_SLOTS], 1)

            def group(it, k, u, items):
                pe.wait_ge(v_in[u], k * 16 + 16)
                counts = iter(place_items(items))
                x = 0
                n, before = 0, None

                def fill():
                    nonlocal x
                    for _ in range(next(counts)):
                        kind, what = items[x]
                        if kind == "strip":
                            g, s, _, t = STRIPS[what]
                            if g == ORDER[0] and (what == 0 or STRIPS[what - 1][1] != s):
                                pe.wait_ge(stack_in[1 - u][s], (k + u) * (16 * STACK_DMAS) + 16 * STACK_DMAS)
                        item(it, items, x, 1 - u)
                        x += 1

                for g, nth, step in STEPS:
                    if nth == 0:
                        pe.wait_ge(max_in[ORDER.index(g)], it * (16 * PARTS) + 16 * PARTS)
                    for s, tile in enumerate(step):
                        scores(it, u, n + s, tile, g, fill)
                    if before is not None:
                        values(it, u, *before)
                    fill()
                    before = (n, ORDER.index(g), nth == 0, nth == STEPS_OF[g] - 1, step)
                    n += len(step)
                values(it, u, *before)

            for slot in range(PROB_SLOTS):
                pe.sem_inc(probs_used[slot], 1)
            pe.wait_ge(const_in, CONSTS)
            for c in range(NG):
                pe.wait_ge(stack_in[0][c], 16 * STACK_DMAS)
            for sem, value in banks_free:
                pe.wait_ge(sem, value)
            for x in range(len(FIRST_ITEMS)):
                item(None, FIRST_ITEMS, x, 0)
            with pe.Fori(0, (ITERS - 2) // 2) as pair:
                group(pair * 2, pair, 0, ITEMS)
                group(pair * 2 + 1, pair, 1, ITEMS)
            group(ITERS - 2, ITERS // 2 - 1, 0, ITEMS)
            group(ITERS - 1, ITERS // 2 - 1, 1, LAST_ITEMS)

        @block.scalar
        def _(act):
            def copy_out(it, g):
                gn, n = ORDER.index(g), LAST_TILE[g]
                act.wait_ge(probs_used[n % PROB_SLOTS], used_value(it, n) + 1)
                act.wait_ge(out_stored[gn % OUT_BUFS], it * (16 * NG // OUT_BUFS) + 16 * (gn // OUT_BUFS + 1))
                act.copy(out_sb[gn % OUT_BUFS][:], p_out[:]).then_inc(out_copied, 1)

            for slot in range(SCORE_SLOTS):
                act.sem_inc(exp_done[slot], 1)
            act.sem_inc(out_copied, 1)
            with act.Fori(0, ITERS) as it:
                n = 0
                for g, nth, step in STEPS:
                    for tile in step:
                        cols = sum(piece[3] for piece in tile)
                        act.wait_ge(score_ready, it * TILES + n + 1)
                        act.wait_ge(probs_used[n % PROB_SLOTS], used_value(it, n))
                        act.activation(probs[n % PROB_SLOTS][:, 0:cols], p_score[n % SCORE_SLOTS][:, 0:cols], ACT.Exp).then_inc(exp_done[n % SCORE_SLOTS], 1)
                        n += 1
                    if nth == 0 and g != ORDER[0]:
                        copy_out(it, ORDER[ORDER.index(g) - 1])
                copy_out(it, ORDER[-1])

        @block.vector
        def _(dve):
            def chunk_maxima(it, x, g, owner):
                for y in range(max(0, x - STRIP_SLOTS + 1), x + 1):
                    dve.wait_ge(strip_free[y % STRIP_SLOTS], item_value(it, y) + 1)
                done = lambda k: owner * (NG * MAX_STEPS) + ORDER.index(g) * MAX_STEPS + k
                dve.tensor_reduce(neg_max[:], strip_max[:, :, g * BLK:(g + 1) * BLK, 0:g + 1], AX.X, ALU.max, negate=True).then_inc(max_step, 1)
                dve.wait_ge(max_step, done(1))
                dve.tensor_copy(max_parts[:, 0], neg_max[:]).then_inc(max_step, 1)
                dve.wait_ge(max_step, done(2))
                dve.tensor_tensor(max_rest[:], neg_max[:], max_parts[:, 0], ALU.subtract).then_inc(max_step, 1)
                dve.wait_ge(max_step, done(3))
                dve.tensor_copy(max_parts[:, 1], max_rest[:]).then_inc(max_step, 1)
                dve.wait_ge(max_step, done(4))
                dve.tensor_tensor(max_parts[:, 2], max_rest[:], max_parts[:, 1], ALU.subtract).then_inc(max_step, 1)

            def run(it, items, inverse_of=None):
                diagonals = []
                turned = {x: (gn, owner) for x, g, gn, owner in turns(it, items)}
                for x, (kind, what) in enumerate(items):
                    slot = x % STRIP_SLOTS
                    if kind == "turn":
                        gn, owner = turned[x]
                        if it is not None or gn >= 2:
                            dve.wait_ge(max_in[(gn + 2) % NG], (owner + (gn >= 2)) * (16 * PARTS))
                        dve.wait_ge(strip_ready[slot], item_value(it, x))
                        dve.tensor_copy(max_t[gn % 2][:], p_max[slot]).then_inc(strip_free[slot], 1)
                        continue
                    g, s, j, t = STRIPS[what]
                    dve.wait_ge(strip_ready[slot], item_value(it, x))
                    dst = strip_max[:, j, t, s:s + 1]
                    if s < g:
                        dve.tensor_reduce(dst, p_strip[:, slot, :], AX.X, ALU.max).then_inc(strip_free[slot], 1)
                    else:
                        width = strip_width(g, s, t)
                        if len(diagonals) >= 2:
                            y = diagonals[-2]
                            dve.wait_ge(strip_free[y % STRIP_SLOTS], item_value(it, y) + 1)
                        dve.sem_inc(waited_dve, 1)
                        dve.tensor_tensor_reduce(unused[len(diagonals) % 2][:, 0:width], p_strip[:, slot, 0:width], mask[:, CH - width:],
                                                 1.0, -3.0e38, ALU.add, ALU.max, dst).then_inc(strip_free[slot], 1)
                        diagonals.append(x)
                    if what == len(STRIPS) - 1 or STRIPS[what + 1][0] != g:
                        chunk_maxima(it, x, g, 0 if it is None else it + 1)
                    if inverse_of is not None and what == len(STRIPS) // 2:
                        invert(inverse_of)

            def invert(it):
                dve.wait_ge(den_in, it * 16 + 16)
                dve.reciprocal(den_inv[:], den[:]).then_inc(den_inverted, 1)

            for slot in range(STRIP_SLOTS):
                dve.sem_inc(strip_free[slot], 1)
            dve.wait_ge(const_in, CONSTS)
            run(None, FIRST_ITEMS)
            run(0, ITEMS)
            with dve.Fori(1, ITERS - 1) as it:
                run(it, ITEMS, inverse_of=it - 1)
            run(ITERS - 1, LAST_ITEMS)
            invert(ITERS - 2)
            invert(ITERS - 1)


def build_finish(nc, keep, io, scr, w_ternary):
    with ExitStack() as ctx:
        m = Work(nc, ctx)
        w = m.sb("w_proj", [P, KC, C])
        b_proj = m.sb("b_proj", [P, BLK, C])
        ident = m.sb("ident_f", [P, P])
        eps = m.sb("eps", [P, 1])
        num = [m.sb(f"num{u}", [P, KC, CH]) for u in range(2)]
        inv_den = [m.sb(f"inv_den{u}", [P, KC, CH]) for u in range(2)]
        x = [m.sb(f"x{u}", [P, BLK, C]) for u in range(2)]
        xb = [m.sb(f"x_bias{u}", [P, BLK, C]) for u in range(2)]
        y_t = [m.sb(f"y_t{u}", [P, KC, CH]) for u in range(2)]
        pre = [[m.sb(f"pre{k}_{u}", [P, BLK, C]) for u in range(NG)] for k in range(2)]
        stats = [m.sb(f"stats{k}", [P, BLK, 6]) for k in range(2)]
        mv = [[m.sb(f"mean_var{k}_{u}", [P, BLK, 2]) for u in range(2)] for k in range(2)]
        dev = [m.sb(f"dev{k}", [P, BLK]) for k in range(2)]
        inv = [m.sb(f"inv{k}", [P, BLK]) for k in range(2)]
        shift = [m.sb(f"shift{k}", [P, BLK]) for k in range(2)]
        normed = [[m.sb(f"normed{k}_{u}", [P, BLK, C]) for u in range((NG, 2)[k])] for k in range(2)]
        h_t = m.sb("h_t", [P, 2, 2, KC, P])
        p_y = [m.psum(f"p_y{h}", [P, 2, C]) for h in range(2)]
        p_t = [m.psum(f"p_t{h}", [P, 2, KC, P]) for h in range(2)]
        p_f = [m.psum(f"p_f{h}", [P, 2, C]) for h in range(2)]

        w_in, eps_set = keep.sem("w_proj_loaded"), keep.sem("eps_set")
        LOADS = 2 * KC + 1
        chunk_in = keep.sems("chunk_loaded", 2)
        xb_ready, y_ready = keep.sem("x_bias_ready"), keep.sem("y_ready")
        sum_ready = [keep.sems(f"sum{k}_ready", 2) for k in range(2)]
        pre_ready = [keep.sems(f"pre{k}_ready", 2) for k in range(2)]
        stats_ready, mv_ready = keep.sems("stats_ready", 2), keep.sems("mean_var_ready", 2)
        dev_ready, inv_ready, shift_ready = keep.sems("dev_ready", 2), keep.sems("inv_ready", 2), keep.sems("shift_ready", 2)
        normed_ready = [keep.sems(f"normed{k}_ready", 2) for k in range(2)]
        turned, turned_copied = keep.sems("turned", 2), keep.sems("turned_copied", 2)
        result_stored = keep.sems("result_stored", 2)
        waited = keep.sem("waited_for_stats")

        block = ctx.enter_context(nc.Block())
        heads = scr["out"].rearrange("(q r) t -> q r t", r=OUT_ROWS)
        HC = P // D

        def steps(eng, step):
            for c in range(NG):
                step(c, c, lambda lag: c >= lag)
            with eng.Fori(1, B) as b:
                for c in range(NG):
                    step(b * NG + c, c, lambda lag: True)
            for c in range(NG):
                step(B * NG + c, c, lambda lag: c < lag)

        @block.sync
        def _(sp):
            sp.dma_start(w[:], io["w_proj"].rearrange("(k p) n -> p k n", p=P)).then_inc(w_in, 16)
            for a in range(BLK):
                sp.dma_start(b_proj[:, a], row_to_all(io["b_proj"], C)).then_inc(w_in, 16)
            sp.dma_start(ident[:], io["ident_f"]).then_inc(w_in, 16)
            with sp.Fori(0, B) as b:
                for c in range(NG):
                    u = c % 2
                    sp.wait_ge(y_ready, b * NG + c + 1)
                    sp.wait_ge(xb_ready, b * NG + c + 1)
                    for k in range(KC):
                        sp.dma_start(num[u][:, k], heads[bass.ds(b * H + k * HC, HC), 0:D, c * CH:(c + 1) * CH]).then_inc(chunk_in[u], 16)
                        inverses = scr["inv"][bass.ds(b * H + k * HC, HC), c * CH:(c + 1) * CH].unsqueeze(1).broadcast_to([HC, D, CH])
                        sp.dma_start(inv_den[u][:, k], inverses).then_inc(chunk_in[u], 16)
                    sp.dma_start(x[u][:], io["x"][bass.ds(b * T + c * CH, CH)].rearrange("(a p) n -> p a n", p=P)).then_inc(chunk_in[u], 16)

        @block.gpsimd
        def _(pool):
            pool.sem_inc(xb_ready, 2)
            pool.sem_inc(y_ready, 2)
            pool.wait_ge(w_in, 16 * (BLK + 2))
            with pool.Fori(0, B) as b:
                for c in range(NG):
                    u, n = c % 2, b * NG + c
                    pool.wait_ge(chunk_in[u], b * (16 * LOADS * NG // 2) + 16 * LOADS * (c // 2 + 1))
                    pool.wait_ge(pre_ready[0][1], n + 1)
                    pool.tensor_tensor(y_t[u][:], num[u][:], inv_den[u][:], ALU.mult).then_inc(y_ready, 1)
                    pool.tensor_tensor(xb[u][:], x[u][:], b_proj[:], ALU.add).then_inc(xb_ready, 1)

        @block.tensor
        def _(pe):
            def linear(k, source, weights, half):
                for a in range(2):
                    for i in range(KC):
                        mm = pe.matmul((p_y, p_f)[k][half][:, a], source(a, i), weights[:, i], start=(i == 0), stop=(i == KC - 1))
                mm.then_inc(sum_ready[k][half], 1)

            def step(n, c, there):
                if there(3):
                    for half in range(2):
                        pe.wait_ge(normed_ready[0][half], (n - 3) * 2 + 2)
                        pe.wait_ge(turned_copied[half], n - 3 + 1)
                        for a in range(2):
                            for k in range(KC):
                                mm = pe.transpose(p_t[half][:, a, k], normed[0][(c - 3) % NG][:, 2 * half + a, k * P:(k + 1) * P], ident[:])
                        mm.then_inc(turned[half], 1)
                if there(1):
                    pe.wait_ge(y_ready, n - 1 + 3)
                    for half in range(2):
                        pe.wait_ge(pre_ready[0][half], n - 1 + 1 + half)
                        linear(0, lambda a, i: y_t[(c + 1) % 2][:, i, (2 * half + a) * P:(2 * half + a + 1) * P], w, half)
                if there(3):
                    for half in range(2):
                        pe.wait_ge(turned_copied[half], n - 3 + 2)
                        pe.wait_ge(pre_ready[1][half], n - 3 + 1)
                        linear(1, lambda a, i: h_t[:, half, a, i], w_ternary, half)

            pe.wait_ge(w_in, 16 * (BLK + 2))
            steps(pe, step)

        @block.scalar
        def _(act):
            def deviation(k, n, c):
                act.wait_ge(mv_ready[k], n * BLK + BLK)
                act.activation(dev[k][:], mv[k][c % 2][:, :, 1], ACT.Sqrt, bias=eps[:, 0:1]).then_inc(dev_ready[k], 1)

            def normalise(k, n, c):
                act.wait_ge(shift_ready[k], n + 1)
                if k == 1:
                    act.wait_ge(result_stored[c % 2], (n - c) * 8 + 16 * (c // 2 + 1))
                for a in range(BLK):
                    act.activation(normed[k][c % len(normed[k])][:, a], pre[k][c][:, a], ACT.Identity, bias=shift[k][:, a:a + 1],
                                   scale=inv[k][:, a:a + 1]).then_inc(normed_ready[k][a // 2], 1)

            def step(n, c, there):
                for k, lag in enumerate((2, 4)):
                    if there(lag):
                        deviation(k, n - lag, (c - lag) % NG)
                if there(3):
                    for half in range(2):
                        act.wait_ge(pre_ready[1][half], n - 3 + 1)
                        act.wait_ge(turned[half], n - 3 + 1)
                        act.copy(h_t[:, half], p_t[half][:]).then_inc(turned_copied[half], 1)
                for k, lag in enumerate((2, 4)):
                    if there(lag):
                        normalise(k, n - lag, (c - lag) % NG)
                if there(4):
                    for half in range(2):
                        act.wait_ge(normed_ready[1][half], (n - 4) * 2 + 2)
                    act.dma_start(io["out"][bass.ds((n - 4) * CH, CH)].rearrange("(a p) n -> p a n", p=P),
                                  normed[1][c % 2][:]).then_inc(result_stored[c % 2], 16)

            for half in range(2):
                act.sem_inc(turned_copied[half], 1)
            for u in range(2):
                act.sem_inc(result_stored[u], 16)
            act.wait_ge(eps_set, 1)
            steps(act, step)
            for u in range(2):
                act.wait_ge(result_stored[u], 16 * (B * NG // 2 + 1))

        @block.vector
        def _(dve):
            def add_and_measure(k, n, c):
                bank, other = ((p_y, xb), (p_f, normed[0]))[k]
                given = lambda half: 2 if k == 0 and half == 1 else 1
                if k == 0:
                    dve.wait_ge(xb_ready, n + 3)
                for half in range(2):
                    dve.wait_ge(sum_ready[k][half], n + 1)
                    dve.tensor_tensor(pre[k][c][:, 2 * half:2 * half + 2], bank[half][:], other[c % len(other)][:, 2 * half:2 * half + 2],
                                      ALU.add).then_inc(pre_ready[k][half], 1)
                for a in range(BLK):
                    dve.wait_ge(pre_ready[k][a // 2], n + given(a // 2) + 1)
                    dve.bn_stats(stats[k][:, a], pre[k][c][:, a]).then_inc(stats_ready[k], 1)
                for a in range(BLK):
                    dve.wait_ge(stats_ready[k], n * BLK + a + 1)
                    dve.sem_inc(waited, 1)
                    dve.bn_aggr(mv[k][c % 2][:, a], stats[k][:, a]).then_inc(mv_ready[k], 1)

            def scale_and_shift(k, n, c):
                dve.wait_ge(dev_ready[k], n + 1)
                dve.reciprocal(inv[k][:], dev[k][:]).then_inc(inv_ready[k], 1)
                dve.wait_ge(inv_ready[k], n + 1)
                dve.scalar_tensor_tensor(out=shift[k][:], in0=mv[k][c % 2][:, :, 0], scalar=-1.0, in1=inv[k][:],
                                         op0=ALU.mult, op1=ALU.mult).then_inc(shift_ready[k], 1)

            def step(n, c, there):
                for k, lag in enumerate((2, 4)):
                    if there(lag):
                        scale_and_shift(k, n - lag, (c - lag) % NG)
                for k, lag in enumerate((1, 3)):
                    if there(lag):
                        add_and_measure(k, n - lag, (c - lag) % NG)

            dve.sem_inc(pre_ready[0][0], 1)
            dve.sem_inc(pre_ready[0][1], 2)
            for half in range(2):
                dve.sem_inc(pre_ready[1][half], 1)
            dve.memset(eps[:], EPS).then_inc(eps_set, 1)
            steps(dve, step)


def build(nc, io):
    scr = {
        "q": nc.dram_tensor("q_parts", (B, PARTS, D, H, T), BF16, kind="Internal").ap(),
        "k": nc.dram_tensor("k_parts", (B, PARTS, D, H, T), BF16, kind="Internal").ap(),
        "v": nc.dram_tensor("v_extended", (ITERS, P, NT, VW), F32, kind="Internal").ap(),
        "out": nc.dram_tensor("attention_sums", (ITERS * P, T), F32, kind="Internal").ap(),
        "inv": nc.dram_tensor("inverse_denominators", (B * H, T), F32, kind="Internal").ap(),
    }
    with ExitStack() as ctx:
        keep = Work(nc, ctx)
        w_ternary = keep.sb("w_ternary", [P, KC, C])
        build_attend(nc, keep, io, scr, w_ternary)
        build_finish(nc, keep, io, scr, w_ternary)


def kernel(L0_attn_x, L0_attn_W_attn, L0_attn_b_attn, L0_attn_W_proj, L0_attn_b_proj, L0_attn_temperature, L0_ffn_weight):
    import ml_dtypes
    import concourse.bacc as bacc
    from concourse.bass_utils import run_bass_kernel_spmd

    x = np.ascontiguousarray(L0_attn_x).reshape(B * T, C)
    w_attn = np.asarray(L0_attn_W_attn)
    w_qk = w_attn[:, :2 * C].reshape(C, 2, H, D).transpose(0, 1, 3, 2).reshape(C, 2 * C)
    b_attn = np.asarray(L0_attn_b_attn)
    b_qk = b_attn[:2 * C].reshape(2, H, D).transpose(0, 2, 1).reshape(2 * KC, P)
    alibi, fixed_rows, tri, mask, ident = constants(np.dtype(ml_dtypes.bfloat16))
    arrays = {
        "x": x,
        "x_t": np.ascontiguousarray(x.T),
        "w_attn": np.concatenate([w_qk, w_attn[:, 2 * C:]], axis=1),
        "b_qk": np.ascontiguousarray(b_qk.T),
        "b_v": np.ascontiguousarray(b_attn[2 * C:]),
        "w_proj": np.ascontiguousarray(L0_attn_W_proj),
        "b_proj": np.ascontiguousarray(L0_attn_b_proj),
        "temperature": np.ascontiguousarray(L0_attn_temperature),
        "w_ffn_t": np.ascontiguousarray(np.asarray(L0_ffn_weight).T),
        "alibi": alibi,
        "fixed_rows": fixed_rows,
        "tri": tri,
        "mask": mask,
        "ident": ident.astype(tri.dtype),
        "ident_f": ident,
    }
    nc = bacc.Bacc("TRN2", target_bir_lowering=False, num_devices=1)
    io = {name: nc.dram_tensor(f"in_{name}", a.shape, mybir.dt.from_np(a.dtype), kind="ExternalInput").ap() for name, a in arrays.items()}
    io["out"] = nc.dram_tensor("out", (B * T, C), F32, kind="ExternalOutput").ap()
    build(nc, io)
    r = run_bass_kernel_spmd(nc, [{f"in_{name}": a for name, a in arrays.items()}], core_ids=[0])
    return r.results[0]["out"].reshape(B, T, C)
```
